# Optimizing a Trainium2 kernel written in Bass

```python
import numpy as np
import jax
import jax.numpy as jnp

def _softmax(x, axis=-1):
    return jax.nn.softmax(x, axis=axis)

def _gelu(x):
    return jax.nn.gelu(x, approximate=True)

def _silu(x):
    return jax.nn.silu(x)

def _sigmoid(x):
    return jax.nn.sigmoid(x)

def _layernorm(x, axis=-1, eps=1e-05):
    m = jnp.mean(x, axis=axis, keepdims=True)
    v = jnp.var(x, axis=axis, keepdims=True)
    return (x - m) / jnp.sqrt(v + eps)

def _scatter_add(tgt, idx, src, axis=0):
    return tgt.at[idx].add(src)

def _segment_sum(src, seg, n):
    return jax.ops.segment_sum(src, seg, n)
kernel_name = 'mk_adj_preln_d2_adj_r2_5b7474'

def setup_inputs(seed: int=0):
    np.random.seed(seed)
    _w = jnp.asarray

    def _rec_inputs():
        import jax
        import jax.numpy as jnp
        _gk = jax.random.key(seed)
        x = -0.000929 + 1 * jax.random.normal(jax.random.fold_in(_gk, 1), (4096, 128), jnp.float32)
        _w = (1.0 + jnp.arange(4096, dtype=jnp.float32)) ** (-0.5)
        _w = _w / _w.mean()
        _pij = jnp.clip(0.000976562 * _w[:, None] * _w[None, :], 0.0, 1.0)
        _a = jax.random.uniform(jax.random.fold_in(_gk, 2), (4096, 4096)) < _pij
        adj = _a.astype(jnp.int32)
        return (x, adj)
    x, adj = _rec_inputs()

    def _L0_gnn_setup():
        import jax, jax.numpy as jnp
        import numpy as np
        NEG_INF = -9000000000000000.0
        ALPHA = 0.2
        key = jax.random.key(seed)
        k1, k2, k3, k4 = jax.random.split(key, 4)
        N, F_IN, H, D = (4096, 128, 4, 32)
        h = jax.random.normal(k1, (N, F_IN), dtype=jnp.float32)
        adj = jax.random.randint(k2, (N, N), 0, 2, dtype=jnp.int32)
        W = jax.random.normal(k3, (F_IN, H * D), dtype=jnp.float32) * (1.0 / np.sqrt(F_IN))
        a = jax.random.normal(k4, (1, H, 2 * D), dtype=jnp.float32)
        return {'h': h, 'adj': adj, 'W': W, 'a': a}
    _L0_gnn_all = _L0_gnn_setup()
    _L0_gnn_in = {k: v for k, v in _L0_gnn_all.items() if k in ('W', 'a')}
    del _L0_gnn_all

    def _L1_gnn_setup():
        import jax, jax.numpy as jnp
        import numpy as np
        from jax import lax
        N = 4096
        D = 128
        CHUNK = 128
        key = jax.random.key(seed)
        k1, k2 = jax.random.split(key)
        x = jax.random.normal(k1, (N, D), dtype=jnp.float32)
        adj = jax.random.randint(k2, (N, N), 0, 2, dtype=jnp.int32)
        return {'x': x, 'adj': adj}
    _L1_gnn_all = _L1_gnn_setup()
    _L1_gnn_in = {k: v for k, v in _L1_gnn_all.items() if k in ()}
    del _L1_gnn_all
    return {'x': x, 'adj': adj, 'L0_gnn_W': _L0_gnn_in['W'], 'L0_gnn_a': _L0_gnn_in['a']}

def reference(x, adj, L0_gnn_W, L0_gnn_a):
    import jax
    import jax.numpy as jnp

    def _L0_gnn_ref(h, adj, W, a):
        import jax, jax.numpy as jnp
        import numpy as np
        NEG_INF = -9000000000000000.0
        ALPHA = 0.2
        N = h.shape[0]
        H = a.shape[1]
        D = a.shape[2] // 2
        Wh = (h @ W).reshape(N, H, D)
        a_src = a[0, :, :D]
        a_dst = a[0, :, D:]
        s_src = jnp.einsum('nhd,hd->nh', Wh, a_src)
        s_dst = jnp.einsum('nhd,hd->nh', Wh, a_dst)
        e = s_src[:, None, :] + s_dst[None, :, :]
        e = jnp.where(e >= 0, e, ALPHA * e)
        e = jnp.where(adj[:, :, None] > 0, e, NEG_INF)
        attention = jax.nn.softmax(e, axis=1)
        h_prime = jnp.einsum('ijh,jhd->ihd', attention, Wh)
        return jax.nn.elu(h_prime.reshape(N, H * D))

    def _L1_gnn_ref(x, adj):
        import jax, jax.numpy as jnp
        import numpy as np
        from jax import lax
        N = 4096
        D = 128
        CHUNK = 128
        n, d = x.shape
        neg = jnp.finfo(x.dtype).min
        adj_chunks = adj.reshape(n // CHUNK, CHUNK, n)

        def step(carry, a):
            mask = a != 0
            masked = jnp.where(mask[:, :, None], x[None, :, :], neg)
            m = jnp.max(masked, axis=1)
            has_nbr = jnp.any(mask, axis=1)
            out = jnp.where(has_nbr[:, None], m, jnp.zeros((), x.dtype))
            return (carry, out)
        _, out = lax.scan(step, None, adj_chunks)
        return out.reshape(n, d)
    h = jnp.maximum(_layernorm(x, axis=-1), 0.0)
    x = x + _L0_gnn_ref(h, adj, L0_gnn_W, L0_gnn_a)
    h = jnp.maximum(_layernorm(x, axis=-1), 0.0)
    x = x + _L1_gnn_ref(h, adj)
    return x

_drawn_inputs = setup_inputs


def setup_inputs(seed=0):
    import zlib

    import numpy as np

    out = dict(_drawn_inputs(seed))
    spreads = {}
    factors = {}
    for name, (base, spread) in spreads.items():
        noise = np.random.default_rng([zlib.crc32(name.encode()), seed]).standard_normal(out[name].shape)
        drawn = base * np.exp(spread * noise) if base else spread * noise
        out[name] = jnp.asarray(drawn.astype(out[name].dtype))
    for name, factor in factors.items():
        out[name] = (out[name] * factor).astype(out[name].dtype)
    return out
```

```python
from contextlib import ExitStack

import concourse.bass as bass
from concourse import mybir

F32 = mybir.dt.float32
I32 = mybir.dt.int32
ALU = mybir.AluOpType
ACT = mybir.ActivationFunctionType
AX = mybir.AxisListType.X
P = 128
ALPHA = 0.2
NEG_INF = -9000000000000000.0
EPS = 1e-05


class Chain:

    def __init__(self, eng, sem, base=0):
        self.eng, self.sem, self.base, self.n = eng, sem, base, 0

    def step(self, ins):
        self.n += 1
        ins.then_inc(self.sem, 1)
        self.eng.wait_ge(self.sem, self.base + self.n)


def gnn_kernel(nc, x, adj, W, a, out):
    N, D = x.shape
    H = a.shape[1]
    HD = a.shape[2] // 2
    T = N // P
    TG = 4
    NGRP = T // TG
    WX = D + 2 * H
    x_v = x.rearrange("(t p) d -> p t d", p=P)
    out_v = out.rearrange("(t p) d -> p t d", p=P)

    with ExitStack() as top:
        def sb(name, shape, dt=F32):
            return top.enter_context(nc.sbuf_tensor(name, shape, dt))

        ps = top.enter_context(nc.psum_tensor("ps", [P, 8, 512], F32))
        ident = sb("ident", [P, P])
        wx = sb("wx", [P, WX])
        abc = sb("abc", [P, 2 * D])
        wa = sb("wa", [P, H, 2, HD])
        wab = sb("wab", [P, H, P])
        xs = sb("xs", [P, T, D])
        hn = sb("hn", [P, T, D])
        hT = sb("hT", [P, N])
        whx = sb("whx", [P, T, WX])
        st = sb("st", [P, 4, T])
        tb = sb("tb", [P, H, N])
        adjt = sb("adjt", [P, N], I32)
        negm = sb("negm", [P, N])
        u = sb("u", [P, N])
        pT = sb("pT", [P, 2, 512])
        scur = sb("scur", [P, H])
        nmax = sb("nmax", [P, H])
        rsum = sb("rsum", [P, H])
        rinv = sb("rinv", [P, H])
        hp = sb("hp", [P, D])
        pooled = sb("pooled", [P, 8])

        def layernorm(tag, load_x):
            with ExitStack() as ctx:
                def sem(name):
                    return ctx.enter_context(nc.semaphore(f"{tag}_{name}"))
                x_in = sem("x_in"); w_in = sem("w_in"); chain = sem("chain"); id0 = sem("id0"); id1 = sem("id1")
                sq_done = sem("sq_done"); var_ready = sem("var_ready"); std_ready = sem("std_ready")
                centred = sem("centred"); h_ready = sem("h_ready")
                tr_done = sem("tr_done"); hT_ready = sem("hT_ready")
                wx_ready = sem("wx_ready"); mm_done = sem("mm_done"); whx_ready = sem("whx_ready")
                block = ctx.enter_context(nc.Block(tag))

                @block.sync
                def _(sp):
                    if load_x:
                        sp.dma_start(wx[:, 0:D], W).then_inc(w_in, 16)
                        sp.dma_start(abc[:, :], a.rearrange("o h k -> o (h k)").broadcast_to([P, 2 * D])).then_inc(w_in, 16)
                        sp.dma_start(xs[:, :, :], x_v).then_inc(x_in, 16)

                @block.gpsimd
                def _(pool):
                    if load_x:
                        nc.gpsimd.memset(ident[:, :], 0.0).then_inc(id0, 1)
                        pool.wait_ge(id0, 1)
                        nc.gpsimd.affine_select(out=ident[:, :], in_=ident[:, :], compare_op=ALU.not_equal, fill=1.0,
                                                base=0, pattern=[[-1, P]], channel_multiplier=1).then_inc(id1, 1)

                G = 8
                NC_ = T // G

                @block.vector
                def _(dve):
                    ch = Chain(dve, chain)
                    if load_x:
                        dve.wait_ge(w_in, 32)
                        for k in range(2):
                            ch.step(nc.vector.tensor_tensor(
                                wa[:, :, k, :], abc[:, :].rearrange("p (h s d) -> p h s d", h=H, s=2)[:, :, k, :],
                                wx[:, 0:D].rearrange("p (h d) -> p h d", h=H), ALU.mult))
                        nc.vector.tensor_reduce(wx[:, D:D + H], wa[:, :, 1, :], AX, ALU.add).then_inc(wx_ready, 1)
                        nc.vector.tensor_reduce(wx[:, D + H:D + 2 * H], wa[:, :, 0, :], AX, ALU.add).then_inc(wx_ready, 1)
                        dve.wait_ge(wx_ready, 2)
                        nc.vector.tensor_copy(wab[:, :, :], wx[:, D:D + H].rearrange("p (h o) -> p h o", o=1).broadcast_to([P, H, P])).then_inc(wx_ready, 1)
                        dve.wait_ge(x_in, 16)
                    for c in range(NC_):
                        g = slice(c * G, c * G + G)
                        ch.step(nc.vector.tensor_reduce(st[:, 0, g], xs[:, g, :], AX, ALU.add))
                        ch.step(nc.vector.tensor_scalar(st[:, 0, g], st[:, 0, g], 1.0 / D, None, ALU.mult))
                        nc.vector.tensor_tensor(hn[:, g, :], xs[:, g, :],
                                                st[:, 0, g].rearrange("p (t o) -> p t o", o=1).broadcast_to([P, G, D]),
                                                ALU.subtract).then_inc(centred, 1)
                        dve.wait_ge(sq_done, c + 1)
                        ch.step(nc.vector.tensor_reduce(st[:, 1, g], u[:, c * G * D:(c + 1) * G * D].rearrange("p (t d) -> p t d", d=D), AX, ALU.add))
                        nc.vector.tensor_scalar(st[:, 2, g], st[:, 1, g], 1.0 / D, EPS, ALU.mult, ALU.add).then_inc(var_ready, 1)
                        dve.wait_ge(std_ready, c + 1)
                        ch.step(nc.vector.reciprocal(st[:, 2, g], st[:, 3, g]))
                        nc.vector.scalar_tensor_tensor(
                            out=hn[:, g, :], in0=hn[:, g, :], scalar=0.0,
                            in1=st[:, 2, g].rearrange("p (t o) -> p t o", o=1).broadcast_to([P, G, D]),
                            op0=ALU.max, op1=ALU.mult).then_inc(h_ready, 1)

                @block.scalar
                def _(act):
                    for c in range(NC_):
                        g = slice(c * G, c * G + G)
                        act.wait_ge(centred, c + 1)
                        nc.scalar.activation(u[:, c * G * D:(c + 1) * G * D], hn[:, g, :].rearrange("p t d -> p (t d)"),
                                             ACT.Square).then_inc(sq_done, 1)
                        act.wait_ge(var_ready, c + 1)
                        nc.scalar.activation(st[:, 3, g], st[:, 2, g], ACT.Sqrt).then_inc(std_ready, 1)
                    for g in range(NGRP):
                        act.wait_ge(tr_done, g + 1)
                        nc.scalar.copy(hT[:, g * 512:(g + 1) * 512], ps[:, g % 2, :]).then_inc(hT_ready, 1)
                        if load_x:
                            act.wait_ge(mm_done, g + 1)
                            nc.scalar.copy(whx[:, g * TG:g * TG + TG, :].rearrange("p (b k) w -> p b (k w)", b=2),
                                           ps[:, 2 + 2 * (g % 2):4 + 2 * (g % 2), 0:2 * WX]).then_inc(whx_ready, 1)
                    if load_x:
                        for h in range(H):
                            for c in range(N // 512):
                                act.wait_ge(mm_done, NGRP + h * (N // 512) + c + 1)
                                nc.scalar.copy(tb[:, h, c * 512:(c + 1) * 512], ps[:, 6 + c % 2, :]).then_inc(whx_ready, 1)

                @block.tensor
                def _(pe):
                    if load_x:
                        pe.wait_ge(id1, 1)
                        pe.wait_ge(wx_ready, 3)
                    for g in range(NGRP):
                        pe.wait_ge(h_ready, g * TG // G + 1)
                        if g >= 2:
                            pe.wait_ge(hT_ready, g - 1)
                        for k in range(TG):
                            last = nc.tensor.transpose(ps[:, g % 2, k * P:(k + 1) * P], hn[:, g * TG + k, :], ident[:, :])
                        last.then_inc(tr_done, 1)
                        if load_x:
                            pe.wait_ge(hT_ready, g + 1)
                            if g >= 2:
                                pe.wait_ge(whx_ready, g - 1)
                            for k in range(TG):
                                last = nc.tensor.matmul(ps[:, 2 + 2 * (g % 2) + k // 2, (k % 2) * WX:(k % 2 + 1) * WX],
                                                        hT[:, (g * TG + k) * P:(g * TG + k + 1) * P], wx[:, :], start=True, stop=True)
                            last.then_inc(mm_done, 1)
                    if load_x:
                        for h in range(H):
                            for c in range(N // 512):
                                n = h * (N // 512) + c
                                if n >= 2:
                                    pe.wait_ge(whx_ready, NGRP + n - 1)
                                nc.tensor.matmul(ps[:, 6 + c % 2, :], wab[:, h, :], hT[:, c * 512:(c + 1) * 512],
                                                 start=True, stop=True).then_inc(mm_done, 1)

        def dense_attention():
            with ExitStack() as ctx:
                def sem(name):
                    return ctx.enter_context(nc.semaphore(f"g0_{name}"))
                adj_in = sem("adj_in"); x_in = sem("x_in"); chain = sem("chain"); e_ready = sem("e_ready"); p_ready = sem("p_ready")
                pT_done = sem("pT_done"); pT_ready = sem("pT_ready"); acc_done = sem("acc_done"); tile_done = sem("tile_done")
                elu_in = sem("elu_in"); elu_out = sem("elu_out")
                block = ctx.enter_context(nc.Block("g0"))
                C = T // 4
                STEPS = 2 + H * 6 + 4

                @block.sync
                def _(sp):
                    with sp.Fori(0, T) as t:
                        sp.wait_ge(tile_done, t + 1)
                        sp.dma_start(adjt[:, :], adj[bass.ds(t * P, P), :]).then_inc(adj_in, 16)

                @block.vector
                def _(dve):
                    nc.vector.memset(hp[:, :], 0.0).then_inc(tile_done, 1)
                    dve.wait_ge(tile_done, 1)
                    with dve.Fori(0, T) as t:
                        ch = Chain(dve, chain, t * STEPS)
                        ch.step(nc.vector.tensor_scalar(scur[:, :], whx[:, bass.ds(t, 1), D + H:D + 2 * H].rearrange("p o h -> p (o h)"), 1.0, None, ALU.mult))
                        dve.wait_ge(adj_in, t * 16 + 16)
                        ch.step(nc.vector.tensor_scalar(negm[:, :], adjt[:, :], -NEG_INF, NEG_INF, ALU.mult, ALU.add))
                        for h in range(H):
                            ch.step(nc.vector.tensor_scalar(u[:, :], tb[:, h, :], scur[:, h:h + 1], None, ALU.add))
                            ch.step(nc.vector.scalar_tensor_tensor(out=u[:, :], in0=u[:, :], scalar=ALPHA, in1=u[:, :],
                                                                   op0=ALU.mult, op1=ALU.max))
                            ch.step(nc.vector.tensor_tensor(u[:, :], u[:, :], adjt[:, :], ALU.mult))
                            ch.step(nc.vector.tensor_tensor(u[:, :], u[:, :], negm[:, :], ALU.add))
                            nc.vector.tensor_reduce(nmax[:, h:h + 1], u[:, :], AX, ALU.max, negate=True).then_inc(e_ready, 1)
                            dve.wait_ge(p_ready, t * H + h + 1)
                            ch.step(nc.vector.reciprocal(rinv[:, h:h + 1], rsum[:, h:h + 1]))
                            dve.wait_ge(acc_done, t * H + h + 1)
                            ch.step(nc.vector.tensor_scalar(hp[:, h * HD:(h + 1) * HD], ps[:, 4, 0:HD], rinv[:, h:h + 1], None, ALU.mult))
                        xt = xs[:, bass.ds(t, 1), :].rearrange("p o d -> p (o d)")
                        nc.vector.tensor_scalar(u[:, 0:D], hp[:, :], 0.0, None, ALU.min).then_inc(elu_in, 1)
                        dve.wait_ge(elu_out, t + 1)
                        ch.step(nc.vector.scalar_tensor_tensor(out=u[:, 0:D], in0=hp[:, :], scalar=0.0, in1=u[:, D:2 * D], op0=ALU.max, op1=ALU.add))
                        ch.step(nc.vector.tensor_scalar(u[:, 0:D], u[:, 0:D], -1.0, None, ALU.add))
                        ch.step(nc.vector.tensor_scalar(hp[:, :], xt, 1.0, None, ALU.mult))
                        ch.step(nc.vector.tensor_tensor(hp[:, :], hp[:, :], u[:, 0:D], ALU.add))
                        nc.vector.tensor_scalar(xt, hp[:, :], 1.0, None, ALU.mult).then_inc(tile_done, 1)
                        dve.wait_ge(tile_done, t + 2)

                @block.scalar
                def _(act):
                    with act.Fori(0, T) as t:
                        for h in range(H):
                            act.wait_ge(e_ready, t * H + h + 1)
                            nc.scalar.activation(u[:, :], u[:, :], ACT.Exp, bias=nmax[:, h:h + 1],
                                                 accum_out=rsum[:, h:h + 1]).then_inc(p_ready, 1)
                            for c in range(C):
                                n = h * C + c
                                act.wait_ge(pT_done, t * (H * C) + n + 1)
                                nc.scalar.copy(pT[:, n % 2, :], ps[:, n % 2, :]).then_inc(pT_ready, 1)
                        act.wait_ge(elu_in, t + 1)
                        nc.scalar.activation(u[:, D:2 * D], u[:, 0:D], ACT.Exp).then_inc(elu_out, 1)

                @block.tensor
                def _(pe):
                    with pe.Fori(0, T) as t:
                        for h in range(H):
                            pe.wait_ge(p_ready, t * H + h + 1)

                            def transposes(c):
                                n = h * C + c
                                for k in range(4):
                                    last = nc.tensor.transpose(ps[:, n % 2, k * P:(k + 1) * P],
                                                               u[:, (c * 4 + k) * P:(c * 4 + k + 1) * P], ident[:, :])
                                last.then_inc(pT_done, 1)

                            transposes(0)
                            for c in range(C):
                                n = h * C + c
                                if c + 1 < C:
                                    if n:
                                        pe.wait_ge(pT_ready, t * (H * C) + n)
                                    transposes(c + 1)
                                pe.wait_ge(pT_ready, t * (H * C) + n + 1)
                                for k in range(4):
                                    j = c * 4 + k
                                    last = nc.tensor.matmul(ps[:, 4, 0:HD], pT[:, n % 2, k * P:(k + 1) * P],
                                                            whx[:, j, h * HD:(h + 1) * HD], start=(j == 0), stop=(j == T - 1))
                            last.then_inc(acc_done, 1)

        def dense_max():
            with ExitStack() as ctx:
                def sem(name):
                    return ctx.enter_context(nc.semaphore(f"g1_{name}"))
                NB = 4
                mask_in = [sem(f"mask_in{b}") for b in range(NB)]
                row_done = sem("row_done"); copied = sem("copied"); tr_done = sem("tr_done"); summed = sem("summed"); out_done = sem("out_done")
                block = ctx.enter_context(nc.Block("g1"))
                outT = negm

                @block.sync
                def _(sp):
                    with sp.Fori(0, N // NB) as i:
                        for b in range(NB):
                            sp.wait_ge(copied, i * NB + NB)
                            sp.dma_start(tb[:, b, :].bitcast(I32), adj[bass.ds(i * NB + b, 1), :].broadcast_to([P, N])).then_inc(mask_in[b], 16)
                    sp.wait_ge(summed, T)
                    sp.dma_start(out_v, hn[:, :, :]).then_inc(out_done, 16)
                    sp.wait_ge(out_done, 16)

                @block.vector
                def _(dve):
                    nc.vector.memset(pooled[:, 0:NB], 0.0).then_inc(copied, NB)
                    dve.wait_ge(copied, NB)
                    with dve.Fori(0, N // NB) as i:
                        for b in range(NB):
                            dve.wait_ge(mask_in[b], i * 16 + 16)
                            nc.vector.memset(pooled[:, NB:NB + 1], 0.0)
                            nc.vector.tensor_tensor_reduce(out=u[:, :], in0=hT[:, :], in1=tb[:, b, :].bitcast(I32), scale=1.0, scalar=0.0,
                                                           op0=ALU.mult, op1=ALU.max, accum_out=pooled[:, b:b + 1]).then_inc(row_done, 1)
                            dve.wait_ge(row_done, i * NB + b + 1)
                        nc.vector.tensor_scalar(outT[:, bass.ds(i * NB, NB)], pooled[:, 0:NB], 1.0, None, ALU.mult).then_inc(copied, NB)
                        dve.wait_ge(copied, i * NB + 2 * NB)
                    for t in range(T):
                        dve.wait_ge(tr_done, t + 1)
                        nc.vector.tensor_tensor(hn[:, t, :], ps[:, t % 4, 0:D], xs[:, t, :], ALU.add).then_inc(summed, 1)

                @block.tensor
                def _(pe):
                    pe.wait_ge(copied, N + NB)
                    for t in range(T):
                        if t >= 4:
                            pe.wait_ge(summed, t - 3)
                        nc.tensor.transpose(ps[:, t % 4, 0:P], outT[:, t * P:(t + 1) * P], ident[:, :]).then_inc(tr_done, 1)

        layernorm("ln0", True)
        dense_attention()
        layernorm("ln1", False)
        dense_max()


_INS = ['x', 'adj', 'L0_gnn_W', 'L0_gnn_a']
_OUTS = [((4096, 128), 'float32')]


def kernel(**inputs):
    import numpy as _np
    import concourse.bacc as _bacc
    from concourse import mybir as _mybir
    from concourse.bass_utils import run_bass_kernel_spmd as _run

    nc = _bacc.Bacc("TRN2", target_bir_lowering=False, num_devices=1)
    arrays, args = {}, []
    for name in _INS:
        a = _np.ascontiguousarray(inputs[name])
        arrays[f"in_{name}_dram"] = a
        args.append(nc.dram_tensor(f"in_{name}_dram", a.shape, _mybir.dt.from_np(a.dtype), kind="ExternalInput").ap())
    for i, (shape, dtype) in enumerate(_OUTS):
        dt = _mybir.dt.from_np(_np.dtype(dtype))
        args.append(nc.dram_tensor(f"out_{i}_dram", shape, dt, kind="ExternalOutput").ap())
    gnn_kernel(nc, *args)
    r = _run(nc, [arrays], core_ids=[0])
    got = tuple(r.results[0][f"out_{i}_dram"] for i in range(len(_OUTS)))
    return got[0]
```

```python
from contextlib import ExitStack

import concourse.bass as bass
from concourse import mybir

F32 = mybir.dt.float32
I32 = mybir.dt.int32
I16 = mybir.dt.int16
BF16 = mybir.dt.bfloat16
ALU = mybir.AluOpType
ACT = mybir.ActivationFunctionType
AX = mybir.AxisListType.X
P = 128
ALPHA = 0.2
NEG_INF = -9000000000000000.0
EPS = 1e-05


class Chain:

    def __init__(self, eng, sem, base=0):
        self.eng, self.sem, self.base, self.n = eng, sem, base, 0

    def step(self, ins):
        self.n += 1
        ins.then_inc(self.sem, 1)
        self.eng.wait_ge(self.sem, self.base + self.n)


def general_path(nc, x, adj, W, a, out):
    N, D = x.shape
    H = a.shape[1]
    HD = a.shape[2] // 2
    T = N // P
    TG = 4
    NGRP = T // TG
    WX = D + 2 * H
    x_v = x.rearrange("(t p) d -> p t d", p=P)
    out_v = out.rearrange("(t p) d -> p t d", p=P)

    with ExitStack() as top:
        def sb(name, shape, dt=F32):
            return top.enter_context(nc.sbuf_tensor(name, shape, dt))

        ps = top.enter_context(nc.psum_tensor("ps", [P, 8, 512], F32))
        ident = sb("ident", [P, P])
        wx = sb("wx", [P, WX])
        abc = sb("abc", [P, 2 * D])
        wa = sb("wa", [P, H, 2, HD])
        wab = sb("wab", [P, H, P])
        xs = sb("xs", [P, T, D])
        hn = sb("hn", [P, T, D])
        hT = sb("hT", [P, N])
        whx = sb("whx", [P, T, WX])
        st = sb("st", [P, 4, T])
        tb = sb("tb", [P, H, N])
        adjt = sb("adjt", [P, N], I32)
        negm = sb("negm", [P, N])
        u = sb("u", [P, N])
        pT = sb("pT", [P, 2, 512])
        scur = sb("scur", [P, H])
        nmax = sb("nmax", [P, H])
        rsum = sb("rsum", [P, H])
        rinv = sb("rinv", [P, H])
        hp = sb("hp", [P, D])
        pooled = sb("pooled", [P, 8])

        def layernorm(tag, load_x):
            with ExitStack() as ctx:
                def sem(name):
                    return ctx.enter_context(nc.semaphore(f"{tag}_{name}"))
                x_in = sem("x_in"); w_in = sem("w_in"); chain = sem("chain"); id0 = sem("id0"); id1 = sem("id1")
                sq_done = sem("sq_done"); var_ready = sem("var_ready"); std_ready = sem("std_ready")
                centred = sem("centred"); h_ready = sem("h_ready")
                tr_done = sem("tr_done"); hT_ready = sem("hT_ready")
                wx_ready = sem("wx_ready"); mm_done = sem("mm_done"); whx_ready = sem("whx_ready")
                block = ctx.enter_context(nc.Block(tag))

                @block.sync
                def _(sp):
                    if load_x:
                        sp.dma_start(wx[:, 0:D], W).then_inc(w_in, 16)
                        sp.dma_start(abc[:, :], a.rearrange("o h k -> o (h k)").broadcast_to([P, 2 * D])).then_inc(w_in, 16)
                        sp.dma_start(xs[:, :, :], x_v).then_inc(x_in, 16)

                @block.gpsimd
                def _(pool):
                    if load_x:
                        nc.gpsimd.memset(ident[:, :], 0.0).then_inc(id0, 1)
                        pool.wait_ge(id0, 1)
                        nc.gpsimd.affine_select(out=ident[:, :], in_=ident[:, :], compare_op=ALU.not_equal, fill=1.0,
                                                base=0, pattern=[[-1, P]], channel_multiplier=1).then_inc(id1, 1)

                G = 8
                NC_ = T // G

                @block.vector
                def _(dve):
                    ch = Chain(dve, chain)
                    if load_x:
                        dve.wait_ge(w_in, 32)
                        for k in range(2):
                            ch.step(nc.vector.tensor_tensor(
                                wa[:, :, k, :], abc[:, :].rearrange("p (h s d) -> p h s d", h=H, s=2)[:, :, k, :],
                                wx[:, 0:D].rearrange("p (h d) -> p h d", h=H), ALU.mult))
                        nc.vector.tensor_reduce(wx[:, D:D + H], wa[:, :, 1, :], AX, ALU.add).then_inc(wx_ready, 1)
                        nc.vector.tensor_reduce(wx[:, D + H:D + 2 * H], wa[:, :, 0, :], AX, ALU.add).then_inc(wx_ready, 1)
                        dve.wait_ge(wx_ready, 2)
                        nc.vector.tensor_copy(wab[:, :, :], wx[:, D:D + H].rearrange("p (h o) -> p h o", o=1).broadcast_to([P, H, P])).then_inc(wx_ready, 1)
                        dve.wait_ge(x_in, 16)
                    for c in range(NC_):
                        g = slice(c * G, c * G + G)
                        ch.step(nc.vector.tensor_reduce(st[:, 0, g], xs[:, g, :], AX, ALU.add))
                        ch.step(nc.vector.tensor_scalar(st[:, 0, g], st[:, 0, g], 1.0 / D, None, ALU.mult))
                        nc.vector.tensor_tensor(hn[:, g, :], xs[:, g, :],
                                                st[:, 0, g].rearrange("p (t o) -> p t o", o=1).broadcast_to([P, G, D]),
                                                ALU.subtract).then_inc(centred, 1)
                        dve.wait_ge(sq_done, c + 1)
                        ch.step(nc.vector.tensor_reduce(st[:, 1, g], u[:, c * G * D:(c + 1) * G * D].rearrange("p (t d) -> p t d", d=D), AX, ALU.add))
                        nc.vector.tensor_scalar(st[:, 2, g], st[:, 1, g], 1.0 / D, EPS, ALU.mult, ALU.add).then_inc(var_ready, 1)
                        dve.wait_ge(std_ready, c + 1)
                        ch.step(nc.vector.reciprocal(st[:, 2, g], st[:, 3, g]))
                        nc.vector.scalar_tensor_tensor(
                            out=hn[:, g, :], in0=hn[:, g, :], scalar=0.0,
                            in1=st[:, 2, g].rearrange("p (t o) -> p t o", o=1).broadcast_to([P, G, D]),
                            op0=ALU.max, op1=ALU.mult).then_inc(h_ready, 1)

                @block.scalar
                def _(act):
                    for c in range(NC_):
                        g = slice(c * G, c * G + G)
                        act.wait_ge(centred, c + 1)
                        nc.scalar.activation(u[:, c * G * D:(c + 1) * G * D], hn[:, g, :].rearrange("p t d -> p (t d)"),
                                             ACT.Square).then_inc(sq_done, 1)
                        act.wait_ge(var_ready, c + 1)
                        nc.scalar.activation(st[:, 3, g], st[:, 2, g], ACT.Sqrt).then_inc(std_ready, 1)
                    for g in range(NGRP):
                        act.wait_ge(tr_done, g + 1)
                        nc.scalar.copy(hT[:, g * 512:(g + 1) * 512], ps[:, g % 2, :]).then_inc(hT_ready, 1)
                        if load_x:
                            act.wait_ge(mm_done, g + 1)
                            nc.scalar.copy(whx[:, g * TG:g * TG + TG, :].rearrange("p (b k) w -> p b (k w)", b=2),
                                           ps[:, 2 + 2 * (g % 2):4 + 2 * (g % 2), 0:2 * WX]).then_inc(whx_ready, 1)
                    if load_x:
                        for h in range(H):
                            for c in range(N // 512):
                                act.wait_ge(mm_done, NGRP + h * (N // 512) + c + 1)
                                nc.scalar.copy(tb[:, h, c * 512:(c + 1) * 512], ps[:, 6 + c % 2, :]).then_inc(whx_ready, 1)

                @block.tensor
                def _(pe):
                    if load_x:
                        pe.wait_ge(id1, 1)
                        pe.wait_ge(wx_ready, 3)
                    for g in range(NGRP):
                        pe.wait_ge(h_ready, g * TG // G + 1)
                        if g >= 2:
                            pe.wait_ge(hT_ready, g - 1)
                        for k in range(TG):
                            last = nc.tensor.transpose(ps[:, g % 2, k * P:(k + 1) * P], hn[:, g * TG + k, :], ident[:, :])
                        last.then_inc(tr_done, 1)
                        if load_x:
                            pe.wait_ge(hT_ready, g + 1)
                            if g >= 2:
                                pe.wait_ge(whx_ready, g - 1)
                            for k in range(TG):
                                last = nc.tensor.matmul(ps[:, 2 + 2 * (g % 2) + k // 2, (k % 2) * WX:(k % 2 + 1) * WX],
                                                        hT[:, (g * TG + k) * P:(g * TG + k + 1) * P], wx[:, :], start=True, stop=True)
                            last.then_inc(mm_done, 1)
                    if load_x:
                        for h in range(H):
                            for c in range(N // 512):
                                n = h * (N // 512) + c
                                if n >= 2:
                                    pe.wait_ge(whx_ready, NGRP + n - 1)
                                nc.tensor.matmul(ps[:, 6 + c % 2, :], wab[:, h, :], hT[:, c * 512:(c + 1) * 512],
                                                 start=True, stop=True).then_inc(mm_done, 1)

        def dense_attention():
            with ExitStack() as ctx:
                def sem(name):
                    return ctx.enter_context(nc.semaphore(f"g0_{name}"))
                adj_in = sem("adj_in"); x_in = sem("x_in"); chain = sem("chain"); e_ready = sem("e_ready"); p_ready = sem("p_ready")
                pT_done = sem("pT_done"); pT_ready = sem("pT_ready"); acc_done = sem("acc_done"); tile_done = sem("tile_done")
                elu_in = sem("elu_in"); elu_out = sem("elu_out")
                block = ctx.enter_context(nc.Block("g0"))
                C = T // 4
                STEPS = 2 + H * 6 + 4

                @block.sync
                def _(sp):
                    with sp.Fori(0, T) as t:
                        sp.wait_ge(tile_done, t + 1)
                        sp.dma_start(adjt[:, :], adj[bass.ds(t * P, P), :]).then_inc(adj_in, 16)

                @block.vector
                def _(dve):
                    nc.vector.memset(hp[:, :], 0.0).then_inc(tile_done, 1)
                    dve.wait_ge(tile_done, 1)
                    with dve.Fori(0, T) as t:
                        ch = Chain(dve, chain, t * STEPS)
                        ch.step(nc.vector.tensor_scalar(scur[:, :], whx[:, bass.ds(t, 1), D + H:D + 2 * H].rearrange("p o h -> p (o h)"), 1.0, None, ALU.mult))
                        dve.wait_ge(adj_in, t * 16 + 16)
                        ch.step(nc.vector.tensor_scalar(negm[:, :], adjt[:, :], -NEG_INF, NEG_INF, ALU.mult, ALU.add))
                        for h in range(H):
                            ch.step(nc.vector.tensor_scalar(u[:, :], tb[:, h, :], scur[:, h:h + 1], None, ALU.add))
                            ch.step(nc.vector.scalar_tensor_tensor(out=u[:, :], in0=u[:, :], scalar=ALPHA, in1=u[:, :],
                                                                   op0=ALU.mult, op1=ALU.max))
                            ch.step(nc.vector.tensor_tensor(u[:, :], u[:, :], adjt[:, :], ALU.mult))
                            ch.step(nc.vector.tensor_tensor(u[:, :], u[:, :], negm[:, :], ALU.add))
                            nc.vector.tensor_reduce(nmax[:, h:h + 1], u[:, :], AX, ALU.max, negate=True).then_inc(e_ready, 1)
                            dve.wait_ge(p_ready, t * H + h + 1)
                            ch.step(nc.vector.reciprocal(rinv[:, h:h + 1], rsum[:, h:h + 1]))
                            dve.wait_ge(acc_done, t * H + h + 1)
                            ch.step(nc.vector.tensor_scalar(hp[:, h * HD:(h + 1) * HD], ps[:, 4, 0:HD], rinv[:, h:h + 1], None, ALU.mult))
                        xt = xs[:, bass.ds(t, 1), :].rearrange("p o d -> p (o d)")
                        nc.vector.tensor_scalar(u[:, 0:D], hp[:, :], 0.0, None, ALU.min).then_inc(elu_in, 1)
                        dve.wait_ge(elu_out, t + 1)
                        ch.step(nc.vector.scalar_tensor_tensor(out=u[:, 0:D], in0=hp[:, :], scalar=0.0, in1=u[:, D:2 * D], op0=ALU.max, op1=ALU.add))
                        ch.step(nc.vector.tensor_scalar(u[:, 0:D], u[:, 0:D], -1.0, None, ALU.add))
                        ch.step(nc.vector.tensor_scalar(hp[:, :], xt, 1.0, None, ALU.mult))
                        ch.step(nc.vector.tensor_tensor(hp[:, :], hp[:, :], u[:, 0:D], ALU.add))
                        nc.vector.tensor_scalar(xt, hp[:, :], 1.0, None, ALU.mult).then_inc(tile_done, 1)
                        dve.wait_ge(tile_done, t + 2)

                @block.scalar
                def _(act):
                    with act.Fori(0, T) as t:
                        for h in range(H):
                            act.wait_ge(e_ready, t * H + h + 1)
                            nc.scalar.activation(u[:, :], u[:, :], ACT.Exp, bias=nmax[:, h:h + 1],
                                                 accum_out=rsum[:, h:h + 1]).then_inc(p_ready, 1)
                            for c in range(C):
                                n = h * C + c
                                act.wait_ge(pT_done, t * (H * C) + n + 1)
                                nc.scalar.copy(pT[:, n % 2, :], ps[:, n % 2, :]).then_inc(pT_ready, 1)
                        act.wait_ge(elu_in, t + 1)
                        nc.scalar.activation(u[:, D:2 * D], u[:, 0:D], ACT.Exp).then_inc(elu_out, 1)

                @block.tensor
                def _(pe):
                    with pe.Fori(0, T) as t:
                        for h in range(H):
                            pe.wait_ge(p_ready, t * H + h + 1)

                            def transposes(c):
                                n = h * C + c
                                for k in range(4):
                                    last = nc.tensor.transpose(ps[:, n % 2, k * P:(k + 1) * P],
                                                               u[:, (c * 4 + k) * P:(c * 4 + k + 1) * P], ident[:, :])
                                last.then_inc(pT_done, 1)

                            transposes(0)
                            for c in range(C):
                                n = h * C + c
                                if c + 1 < C:
                                    if n:
                                        pe.wait_ge(pT_ready, t * (H * C) + n)
                                    transposes(c + 1)
                                pe.wait_ge(pT_ready, t * (H * C) + n + 1)
                                for k in range(4):
                                    j = c * 4 + k
                                    last = nc.tensor.matmul(ps[:, 4, 0:HD], pT[:, n % 2, k * P:(k + 1) * P],
                                                            whx[:, j, h * HD:(h + 1) * HD], start=(j == 0), stop=(j == T - 1))
                            last.then_inc(acc_done, 1)

        def dense_max():
            with ExitStack() as ctx:
                def sem(name):
                    return ctx.enter_context(nc.semaphore(f"g1_{name}"))
                NB = 4
                mask_in = [sem(f"mask_in{b}") for b in range(NB)]
                row_done = sem("row_done"); copied = sem("copied"); tr_done = sem("tr_done"); summed = sem("summed"); out_done = sem("out_done")
                block = ctx.enter_context(nc.Block("g1"))
                outT = negm

                @block.sync
                def _(sp):
                    with sp.Fori(0, N // NB) as i:
                        for b in range(NB):
                            sp.wait_ge(copied, i * NB + NB)
                            sp.dma_start(tb[:, b, :].bitcast(I32), adj[bass.ds(i * NB + b, 1), :].broadcast_to([P, N])).then_inc(mask_in[b], 16)
                    sp.wait_ge(summed, T)
                    sp.dma_start(out_v, hn[:, :, :]).then_inc(out_done, 16)
                    sp.wait_ge(out_done, 16)

                @block.vector
                def _(dve):
                    nc.vector.memset(pooled[:, 0:NB], 0.0).then_inc(copied, NB)
                    dve.wait_ge(copied, NB)
                    with dve.Fori(0, N // NB) as i:
                        for b in range(NB):
                            dve.wait_ge(mask_in[b], i * 16 + 16)
                            nc.vector.memset(pooled[:, NB:NB + 1], 0.0)
                            nc.vector.tensor_tensor_reduce(out=u[:, :], in0=hT[:, :], in1=tb[:, b, :].bitcast(I32), scale=1.0, scalar=0.0,
                                                           op0=ALU.mult, op1=ALU.max, accum_out=pooled[:, b:b + 1]).then_inc(row_done, 1)
                            dve.wait_ge(row_done, i * NB + b + 1)
                        nc.vector.tensor_scalar(outT[:, bass.ds(i * NB, NB)], pooled[:, 0:NB], 1.0, None, ALU.mult).then_inc(copied, NB)
                        dve.wait_ge(copied, i * NB + 2 * NB)
                    for t in range(T):
                        dve.wait_ge(tr_done, t + 1)
                        nc.vector.tensor_tensor(hn[:, t, :], ps[:, t % 4, 0:D], xs[:, t, :], ALU.add).then_inc(summed, 1)

                @block.tensor
                def _(pe):
                    pe.wait_ge(copied, N + NB)
                    for t in range(T):
                        if t >= 4:
                            pe.wait_ge(summed, t - 3)
                        nc.tensor.transpose(ps[:, t % 4, 0:P], outT[:, t * P:(t + 1) * P], ident[:, :]).then_inc(tr_done, 1)

        layernorm("ln0", True)
        dense_attention()
        layernorm("ln1", False)
        dense_max()


def edge_groups(tiles):
    blocks = {1: 11, 2: 9, 3: 7, 4: 7, 5: 6, 6: 6}
    groups = [(0, r, 8, 32, 4, 3) for r in range(8)]
    for t in range(1, tiles):
        b = blocks.get(t, 5 if t < 11 else 4 if t < 21 else 3)
        groups.append((t, 0, 1, 24 if t < 4 else 16, 8 if t < 4 else 4, b))
    return groups


BITS = 8
BIG = 1e30


class Plan:

    def __init__(self, tiles, ring):
        self.groups = edge_groups(tiles)
        self.n = len(self.groups)
        self.tile = [g[0] for g in self.groups]
        self.last = [max(i for i in range(self.n) if self.tile[i] == t) for t in range(tiles)]
        self.first = [min(i for i in range(self.n) if self.tile[i] == t) for t in range(tiles)]
        self.block0, self.at, self.free_after = [], [], []
        owner = [None] * ring
        n = pos = 0
        for i, g in enumerate(self.groups):
            b = g[5]
            self.block0.append(n)
            n += b
            if pos + b > ring:
                pos = 0
            old = [o for o in owner[pos:pos + b] if o is not None]
            self.free_after.append(max(old) + 1 if old else 0)
            owner[pos:pos + b] = [g[0]] * b
            self.at.append(pos)
            pos += b
        self.blocks = n
        for i in range(self.n):
            assert not self.free_after[i] or self.last[self.free_after[i] - 1] <= i - 5

    def ended(self, i):
        return [t for t, l in enumerate(self.last) if l == i]


def edge_path(nc, x, adj, W, a, out, top, missed):
    N, D = x.shape
    H = a.shape[1]
    HD = a.shape[2] // 2
    T = N // P
    WX = D + 2 * H
    C = N // BITS
    RING = 58
    plan = Plan(T, RING)
    NV, NB = plan.n, plan.blocks
    MAXB = max(g[5] for g in plan.groups)
    MAXK = max(g[3] for g in plan.groups)
    MW = 7
    NA = 4
    wh_table = nc.dram_tensor("wh_table", [N, WX], F32).ap()
    h1_table = nc.dram_tensor("h1_table", [N, D], F32).ap()
    x_v = x.rearrange("(t p) d -> p t d", p=P)
    wh_v = wh_table.rearrange("(t p) d -> p t d", p=P)
    h1_v = h1_table.rearrange("(t p) d -> p t d", p=P)
    out_v = out.rearrange("(t p) d -> p t d", p=P)

    def sb(name, shape, dt=F32):
        return top.enter_context(nc.sbuf_tensor(name, shape, dt))

    ps = top.enter_context(nc.psum_tensor("psf", [P, 8, 512], F32))
    ident = sb("identf", [P, P])
    identb = sb("identb", [P, P], BF16)
    iota = sb("iota", [P, MAXB * P], I16)
    xs = sb("xsf", [P, T, D])
    hn = sb("hnf", [P, T, D])
    idx = sb("idx", [P, NB], I32)
    meta = sb("meta", [P, NB, 3])
    kq = sb("kq", [P, NB])
    rowq = sb("rowq", [P, NB])
    last_q = sb("last_q", [P, NB])
    keep = sb("keep", [P, NB])

    def edge_attention():
      with ExitStack() as ctx:
        def sbl(name, shape, dt=F32):
            return ctx.enter_context(nc.sbuf_tensor(name, shape, dt))

        def sem(name):
            return ctx.enter_context(nc.semaphore(name))
        adjt = sbl("adjf", [P, NA, N // 2], I32)
        adjb = sbl("adjb", [P, 2, N], BF16)
        Rm = sbl("Rm", [P, RING, P])
        OQ = sbl("OQ", [P, RING, P])
        G = sbl("G", [P, RING, WX])
        whx = sbl("whxf", [P, 2, 4, WX])
        hc = sbl("hc", [P, 4])
        hTb = G[:, 0:8, 0:P]
        tri = sbl("tri", [P, P])
        packw = sbl("packw", [P, BITS, P], BF16)
        ones_b = sbl("ones_b", [1, P], BF16)
        cnum = sbl("cnum", [1, 2, C], BF16)
        avg = sbl("avg", [P, P])
        maskk = sbl("maskk", [P, BITS], I32)
        kbase = sbl("kbase", [P, BITS])
        qpos = sbl("qpos", [P, MAXB])
        X = sbl("X", [P, 3, MAXK + MW])
        s_all = sbl("s_all", [P, T, H])
        wd = sbl("wd", [P, 64])
        wsel = sbl("wsel", [P, MAXK])
        wi = sbl("wi", [P, 2, MAXK], I32)
        mbuf = sbl("mb", [P, MAXB * 24], I32)
        mb = mbuf[:, 0:MAXK * BITS].rearrange("p (k b) -> p k b", b=BITS)
        jj = sbl("jj", [P, MAXK, BITS])
        valid = sbl("valid", [P, 8, MAXK])
        endr = sbl("endr", [P, 1])
        eq = sbl("eq", [P, 4, MAXB * 24], BF16)
        sq = sbl("sq", [P, RING, H])
        prod = mbuf[:, :].bitcast(F32)
        jq = sbl("jq", [P, MAXB])
        e = sbl("e", [P, RING, H])
        dq = sbl("dq", [P, RING, H])
        E2 = sbl("E2", [P, MAXB * 24 * H])
        em = sbl("em", [P, MAXK, H])
        mv = sbl("mv", [P, 8, H])
        mrow = sbl("mrow", [P, 2, H])
        rc = sbl("rc", [P, T, 2])
        rc2 = sbl("rc2", [P, 1])
        none = sbl("none", [P, T])
        den = sbl("den", [P, H])
        rden = sbl("rden", [P, H])
        hp = sbl("hp_f", [P, D])
        mn = sbl("mn", [P, D])
        ex = sbl("ex", [P, D])
        mwh = sbl("mwh", [P, D])
        stats = sbl("stats", [P, T, 6])
        agg = sbl("agg", [P, T, 2])
        veps = sbl("veps", [P, T])
        rstd = sbl("rstd", [P, T])
        half = sbl("half", [P, T])
        wx = sbl("wxf", [P, WX])
        abc = Rm[:, 0:2, :].rearrange("p a b -> p (a b)")
        wa = Rm[:, 2:4, :].rearrange("p a (h d) -> p h a d", h=H)

        w_in, x_in = sem("w_in"), [sem(f"x_in{c}") for c in range(4)]
        adj_in = [sem(f"adj_in{b}") for b in range(NA)]
        adj_bf, packed, words_used = sem("adj_bf"), sem("packed"), sem("words_used")
        consts, pchain, chain = sem("consts"), sem("pchain"), sem("chain")
        packw_ready, wx_ready = sem("packw_ready"), sem("wx_ready")
        var0_ready, rstd0_ready, c0_ready = sem("var0_ready"), sem("rstd0_ready"), sem("c0_ready")
        tr0_done, hT_ready, mm0_done, whx_ready = sem("tr0_done"), sem("hT_ready"), sem("mm0_done"), sem("whx_ready")
        wh_stored = [sem(f"wh_stored{b}") for b in range(2)]
        mean_done, mean_ready, s_copied = sem("mean_done"), sem("mean_ready"), sem("s_copied")
        x_ready, off_done, r_ready, sel_done, idx_ready = (sem("x_ready"), sem("off_done"), sem("r_ready"),
                                                           sem("sel_done"), sem("idx_ready"))
        gathered = [sem(f"gathered{b}") for b in range(4)]
        e2_ready, rowe_done, max_ready, mback_done = sem("e2_ready"), sem("rowe_done"), sem("max_ready"), sem("mback_done")
        d_ready, p_ready, g_ready, agg_done = sem("d_ready"), sem("p_ready"), sem("g_ready"), sem("agg_done")
        agg_used = sem("agg_used")
        elu_in, elu_out, var1_ready, rstd1_ready = sem("elu_in"), sem("elu_out"), sem("var1_ready"), sem("rstd1_ready")
        c1_ready, h1_ready, h1_stored = sem("c1_ready"), sem("h1_ready"), sem("h1_stored")
        block = ctx.enter_context(nc.Block("edges0"))

        def tile_waits(eng, sems, n):
            eng.wait_ge(sems[n % len(sems)], 16 * (n // len(sems) + 1))

        @block.sync
        def _(sp):
            sp.dma_start(wx[:, 0:D], W).then_inc(w_in, 16)
            sp.dma_start(abc, a.rearrange("o h k -> o (h k)").broadcast_to([P, 2 * D])).then_inc(w_in, 16)
            for c in range(4):
                g = slice(c * T // 4, (c + 1) * T // 4)
                sp.dma_start(xs[:, g, :], x_v[:, g, :]).then_inc(x_in[c], 16)
            stored = 0

            def store_wh(g):
                sp.wait_ge(whx_ready, 4 * g + 4)
                sp.dma_start(wh_v[:, 4 * g:4 * g + 4, :], whx[:, g % 2]).then_inc(wh_stored[g % 2], 16)

            def load_adj(m):
                if m >= NA:
                    sp.wait_ge(adj_bf, m - NA + 1)
                t, c = m // 2, (m % 2) * (N // 2)
                sp.dma_start(adjt[:, m % NA, :], adj[t * P:(t + 1) * P, c:c + N // 2]).then_inc(adj_in[m % NA], 16)

            for m in range(NA):
                load_adj(m)
            for g in range(T // 4):
                store_wh(g)
            for m in range(NA, 2 * T):
                load_adj(m)

        @block.gpsimd
        def _(pool):
            ch = Chain(pool, pchain)
            ch.step(nc.gpsimd.memset(ident[:, :], 0.0))
            nc.gpsimd.affine_select(out=ident[:, :], in_=ident[:, :], compare_op=ALU.not_equal, fill=1.0,
                                    base=0, pattern=[[-1, P]], channel_multiplier=1).then_inc(consts, 1)
            nc.gpsimd.memset(half[:, :], -0.5).then_inc(consts, 1)
            pool.wait_ge(consts, 2)
            for k in range(BITS):
                nc.gpsimd.memset(maskk[:, k:k + 1], 1 << (9 + k)).then_inc(consts, 1)
            nc.gpsimd.iota(kbase[:, :], pattern=[[C, BITS]], base=1, channel_multiplier=0,
                           allow_small_or_imprecise_dtypes=True).then_inc(consts, 1)
            nc.gpsimd.iota(cnum[:, 0, :], pattern=[[0, 2], [1, C // 2]], base=0, channel_multiplier=0,
                           allow_small_or_imprecise_dtypes=True).then_inc(consts, 1)
            nc.gpsimd.iota(cnum[:, 1, :], pattern=[[C // 2, 2], [0, C // 2]], base=0, channel_multiplier=0,
                           allow_small_or_imprecise_dtypes=True).then_inc(consts, 1)
            nc.gpsimd.memset(ones_b[:, :], 1.0).then_inc(consts, 1)
            nc.gpsimd.iota(qpos[:, :], pattern=[[P, MAXB]], base=0, channel_multiplier=1,
                           allow_small_or_imprecise_dtypes=True).then_inc(consts, 1)
            nc.gpsimd.iota(iota[:, :], pattern=[[1, MAXB * P]], base=0, channel_multiplier=0,
                           allow_small_or_imprecise_dtypes=True).then_inc(consts, 1)
            for b in range(3):
                nc.gpsimd.iota(X[:, b, MAXK + 2:MAXK + 3], pattern=[[0, 1]], base=1, channel_multiplier=1,
                               allow_small_or_imprecise_dtypes=True).then_inc(consts, 1)
            ch.step(nc.gpsimd.memset(tri[:, :], 1.0))
            nc.gpsimd.affine_select(out=tri[:, :], in_=tri[:, :], compare_op=ALU.is_gt, fill=0.0,
                                    base=0, pattern=[[1, P]], channel_multiplier=-1).then_inc(consts, 1)
            nc.gpsimd.memset(avg[:, :], 1.0 / N).then_inc(consts, 1)
            for c in range(4):
                g = slice(c * T // 4, (c + 1) * T // 4)
                pool.wait_ge(var0_ready, c + 1)
                nc.gpsimd.tensor_tensor(rstd[:, g], veps[:, g], half[:, g], ALU.pow).then_inc(rstd0_ready, 1)
            for b in range(2):
                pool.wait_ge(wh_stored[b], 16 * (T // 8))
            for i in range(NV + 6):
                if i < NV:
                    t, r, F, K, GR, B = plan.groups[i]
                    pool.wait_ge(idx_ready, i + 1)
                    if plan.free_after[i]:
                        pool.wait_ge(agg_done, plan.free_after[i])
                    for b in range(B):
                        n = plan.block0[i] + b
                        pool.indirect_dma_start(G[:, plan.at[i] + b, :], None, wh_table,
                                                bass.IndirectOffsetOnAxis(ap=idx[:, n:n + 1], axis=0)
                                                ).then_inc(gathered[i % 4], 16)
                for t in plan.ended(i - 6):
                    pool.wait_ge(var1_ready, t + 1)
                    nc.gpsimd.tensor_tensor(rstd[:, t:t + 1], veps[:, t:t + 1], half[:, t:t + 1], ALU.pow
                                            ).then_inc(rstd1_ready, 1)

        gat_total = [0] * 4
        gat_need = []
        for i in range(NV):
            gat_total[i % 4] += 16 * plan.groups[i][5]
            gat_need.append(gat_total[i % 4])
        NCONST = 2 + BITS + 6 + 3 + 2

        @block.scalar
        def _(act):
            def convert(t):
                for m in (2 * t, 2 * t + 1):
                    tile_waits(act, adj_in, m)
                    if m % 2 == 0 and t >= 2:
                        act.wait_ge(packed, t - 1)
                    c = (m % 2) * (N // 2)
                    nc.scalar.activation(adjb[:, t % 2, c:c + N // 2], adjt[:, m % NA, :], ACT.Copy,
                                         accum_out=rc[:, t, m % 2:m % 2 + 1]).then_inc(adj_bf, 1)

            convert(0)
            for g in range(T // 4):
                act.wait_ge(tr0_done, g + 1)
                nc.scalar.copy(hTb[:, 4 * (g % 2):4 * (g % 2) + 4, :], ps[:, g % 2, :].rearrange("p (k q) -> p k q", k=4)
                               ).then_inc(hT_ready, 1)
                act.wait_ge(mm0_done, g + 1)
                if g % 2 == 0:
                    act.wait_ge(rstd0_ready, g // 2 + 1)
                if g >= 2:
                    act.wait_ge(wh_stored[g % 2], 16 * (g // 2))
                    act.wait_ge(mean_done, g - 1)
                    act.wait_ge(s_copied, g - 1)
                for k in range(4):
                    t = 4 * g + k
                    w = ps[:, 2 + 2 * (g % 2) + k // 2, (k % 2) * WX:(k % 2 + 1) * WX]
                    nc.scalar.activation(whx[:, g % 2, k, :], w, ACT.Copy, scale=rstd[:, t:t + 1]).then_inc(whx_ready, 1)
            act.wait_ge(mean_done, T // 4)
            nc.scalar.copy(mwh[:, :], ps[:, 7, 0:D]).then_inc(mean_ready, 1)
            convert(1)
            for i in range(NV + 7):
                for t in plan.ended(i - 4):
                    for v in range(plan.first[t], plan.last[t] + 1):
                        B, at = plan.groups[v][5], plan.at[v]
                        act.wait_ge(d_ready, v + 1)
                        nc.scalar.activation(G[:, at:at + B, D:D + H], dq[:, at:at + B, :], ACT.Exp).then_inc(p_ready, 1)
                if i < NV and i == plan.first[plan.tile[i]] and plan.tile[i] + 2 < T:
                    convert(plan.tile[i] + 2)
                for t in plan.ended(i - 5):
                    act.wait_ge(elu_in, t + 1)
                    nc.scalar.activation(ex[:, :], mn[:, :], ACT.Exp).then_inc(elu_out, 1)
                for t in plan.ended(i - 6):
                    act.wait_ge(c1_ready, t + 1)
                    act.wait_ge(rstd1_ready, t + 1)
                    nc.scalar.mul(hn[:, t, :], hn[:, t, :], rstd[:, t:t + 1]).then_inc(h1_ready, 1)
                    act.wait_ge(h1_ready, t + 1)
                    act.dma_start(h1_v[:, t, :], hn[:, t, :]).then_inc(h1_stored, 16)
            act.wait_ge(h1_stored, 16 * T)

        @block.tensor
        def _(pe):
            pe.wait_ge(consts, NCONST)
            pe.wait_ge(packw_ready, BITS)

            def pack(t):
                pe.wait_ge(adj_bf, 2 * t + 2)
                if t >= 2:
                    pe.wait_ge(words_used, plan.last[t - 2] + 1)
                o = ps[:, t % 2, :]
                for k in range(BITS):
                    nc.tensor.matmul(o, packw[:, k, :], adjb[:, t % 2, k * C:(k + 1) * C], start=(k == 0), stop=False)
                nc.tensor.matmul(o, ones_b[:, :], cnum[:, 0, :], start=False, stop=False)
                nc.tensor.matmul(o, ones_b[:, :], cnum[:, 1, :], start=False, stop=True).then_inc(packed, 1)

            pe.wait_ge(wx_ready, 2)
            for g in range(T // 4):
                if g % 2 == 0:
                    pe.wait_ge(c0_ready, g // 2 + 1)
                if g >= 2:
                    pe.wait_ge(hT_ready, g - 1)
                for k in range(4):
                    last = nc.tensor.transpose(ps[:, g % 2, k * P:(k + 1) * P], hn[:, 4 * g + k, :], ident[:, :])
                last.then_inc(tr0_done, 1)
                pe.wait_ge(hT_ready, g + 1)
                if g >= 2:
                    pe.wait_ge(whx_ready, 4 * (g - 1))
                for k in range(4):
                    last = nc.tensor.matmul(ps[:, 2 + 2 * (g % 2) + k // 2, (k % 2) * WX:(k % 2 + 1) * WX],
                                            hTb[:, 4 * (g % 2) + k, :], wx[:, :], start=True, stop=True)
                last.then_inc(mm0_done, 1)
                pe.wait_ge(whx_ready, 4 * g + 4)
                for k in range(4):
                    t = 4 * g + k
                    last = nc.tensor.matmul(ps[:, 7, 0:D], avg[:, :], whx[:, g % 2, k, 0:D], start=(t == 0), stop=(t == T - 1))
                last.then_inc(mean_done, 1)
            pack(0)
            for i in range(NV + 5):
                if 0 <= i - 3 < NV:
                    v = i - 3
                    t, r, F, K, GR, B = plan.groups[v]
                    pe.wait_ge(e2_ready, v + 1)
                    for b in range(B):
                        last = nc.tensor.matmul(ps[:, 5, 0:K * H], OQ[:, plan.at[v] + b, :],
                                                E2[:, b * K * H:(b + 1) * K * H], start=(b == 0), stop=(b == B - 1))
                    last.then_inc(rowe_done, 1)
                for t in plan.ended(i - 4):
                    pe.wait_ge(max_ready, t + 1)
                    nblk = 0
                    for v in range(plan.first[t], plan.last[t] + 1):
                        for b in range(plan.groups[v][5]):
                            last = nc.tensor.matmul(ps[:, 4, nblk * H:nblk * H + H], Rm[:, plan.at[v] + b, :],
                                                    mrow[:, t % 2, :], start=True, stop=True)
                            nblk += 1
                    last.then_inc(mback_done, 1)
                if i < NV:
                    t, r, F, K, GR, B = plan.groups[i]
                    pe.wait_ge(x_ready, i + 1)
                    nc.tensor.matmul(ps[:, 4, 256 + i % 2:257 + i % 2], tri[:, :], X[:, i % 3, MAXK + 1:MAXK + 2],
                                     start=True, stop=True).then_inc(off_done, 1)
                    pe.wait_ge(r_ready, i + 1)
                    for b in range(B):
                        last = nc.tensor.matmul(ps[:, 2 + i % 2, b * (K + MW):(b + 1) * (K + MW)], Rm[:, plan.at[i] + b, :],
                                                X[:, i % 3, MAXK - K:MAXK + MW], start=True, stop=True)
                    last.then_inc(sel_done, 1)
                for t in plan.ended(i - 4):
                    for v in range(plan.first[t], plan.last[t] + 1):
                        B = plan.groups[v][5]
                        pe.wait_ge(g_ready, v + 1)
                        if v == plan.first[t] and t >= 2:
                            pe.wait_ge(agg_used, t - 1)
                        for b in range(B):
                            last = nc.tensor.matmul(ps[:, 6 + t % 2, 0:D + H], OQ[:, plan.at[v] + b, :],
                                                    G[:, plan.at[v] + b, 0:D + H],
                                                    start=(v == plan.first[t] and b == 0), stop=(v == plan.last[t] and b == B - 1))
                    last.then_inc(agg_done, 1)
                if i < NV and i == plan.first[plan.tile[i]] and plan.tile[i] + 1 < T:
                    pack(plan.tile[i] + 1)

        @block.vector
        def _(dve):
            ch = Chain(dve, chain)
            step = ch.step
            V = nc.vector
            dve.wait_ge(w_in, 32)
            ab = abc.rearrange("p (h s d) -> p h s d", h=H, s=2)
            for k in range(2):
                step(V.tensor_tensor(wa[:, :, k, :], ab[:, :, k, :], wx[:, 0:D].rearrange("p (h d) -> p h d", h=H), ALU.mult))
            V.tensor_reduce(wx[:, D:D + H], wa[:, :, 1, :], AX, ALU.add).then_inc(wx_ready, 1)
            V.tensor_reduce(wx[:, D + H:D + 2 * H], wa[:, :, 0, :], AX, ALU.add).then_inc(wx_ready, 1)
            dve.wait_ge(consts, NCONST)
            for k in range(BITS):
                V.tensor_scalar(packw[:, k, :], ident[:, :], float(1 << (9 + k)), None, ALU.mult).then_inc(packw_ready, 1)
            V.tensor_copy(identb[:, :], ident[:, :])
            for c in range(4):
                dve.wait_ge(x_in[c], 16)
                for t in range(c * T // 4, (c + 1) * T // 4):
                    step(V.bn_stats(stats[:, t, :], xs[:, t, :]))
                    step(V.bn_aggr(agg[:, t, :], stats[:, t, :]))
                    last = V.tensor_scalar(hn[:, t, :], xs[:, t, :], agg[:, t, 0:1], 0.0, ALU.subtract, ALU.max)
                last.then_inc(c0_ready, 1)
                g = slice(c * T // 4, (c + 1) * T // 4)
                V.tensor_scalar(veps[:, g], agg[:, g, 1], EPS, None, ALU.add).then_inc(var0_ready, 1)

            def extract(i):
                t, r, F, K, GR, B = plan.groups[i]
                dve.wait_ge(packed, t + 1)
                words = ps[:, t % 2, :].rearrange("p (m g f) -> p f g m", g=GR, f=F)
                for g in range(GR):
                    last = V.max(wd[:, g * 8:g * 8 + 8], words[:, r, g, :])
                    if g < GR - 1:
                        last.then_inc(chain, 1)
                        ch.n += 1
                last.then_inc(words_used, 1)
                dve.wait_ge(words_used, i + 1)
                src = wd[:, 0:8 * GR]
                if 8 * GR > K:
                    for q in range(K // 8):
                        step(V.max(wsel[:, 8 * q:8 * q + 8], src))
                        if q < K // 8 - 1:
                            step(V.match_replace(src, wsel[:, 8 * q:8 * q + 8], src, 0.0))
                    src = wsel[:, 0:K]
                step(V.tensor_copy(wi[:, 0, 0:K], src))
                step(V.tensor_scalar(wi[:, 1, 0:K], wi[:, 0, 0:K], C - 1, None, ALU.bitwise_and))
                V.tensor_tensor(mb[:, 0:K, :], wi[:, 0, 0:K].rearrange("p (k o) -> p k o", o=1).broadcast_to([P, K, BITS]),
                                maskk[:, :].rearrange("p (o k) -> p o k", o=1).broadcast_to([P, K, BITS]), ALU.bitwise_and
                                ).then_inc(chain, 1)
                ch.n += 1
                step(V.tensor_tensor(jj[:, 0:K, :], wi[:, 1, 0:K].rearrange("p (k o) -> p k o", o=1).broadcast_to([P, K, BITS]),
                                     kbase[:, :].rearrange("p (o k) -> p o k", o=1).broadcast_to([P, K, BITS]), ALU.add))
                cand = jj[:, 0:K, :].rearrange("p k b -> p (k b)")
                step(V.scalar_tensor_tensor(out=cand, in0=mb[:, 0:K, :].rearrange("p k b -> p (k b)"), scalar=0.0, in1=cand,
                                            op0=ALU.is_gt, op1=ALU.mult))
                k0 = MAXK - K
                Xi = X[:, i % 3, :]
                if i >= 3:
                    dve.wait_ge(sel_done, i - 2)
                for q in range(K // 8):
                    step(V.max(Xi[:, k0 + 8 * q:k0 + 8 * q + 8], cand))
                    if q < K // 8 - 1:
                        step(V.match_replace(cand, Xi[:, k0 + 8 * q:k0 + 8 * q + 8], cand, 0.0))
                step(V.tensor_scalar(valid[:, i % 8, 0:K], Xi[:, k0:MAXK], 0.0, None, ALU.is_gt))
                if i == 0:
                    pass
                V.tensor_copy(Xi[:, MAXK + 3:MAXK + 3 + H], s_all[:, t, :])
                V.tensor_reduce(Xi[:, MAXK + 1:MAXK + 2], valid[:, i % 8, 0:K], AX, ALU.add).then_inc(x_ready, 1)

            def rows_of_edges(i):
                t, r, F, K, GR, B = plan.groups[i]
                Xi = X[:, i % 3, :]
                dve.wait_ge(off_done, i + 1)
                step(V.tensor_copy(Xi[:, MAXK:MAXK + 1], ps[:, 4, 256 + i % 2:257 + i % 2]))
                step(V.tensor_tensor(endr[:, :], Xi[:, MAXK:MAXK + 1], Xi[:, MAXK + 1:MAXK + 2], ALU.add))
                if plan.free_after[i]:
                    dve.wait_ge(agg_done, plan.free_after[i])
                R = Rm[:, plan.at[i]:plan.at[i] + B, :].rearrange("p b q -> p (b q)")
                step(V.tensor_scalar(R, iota[:, 0:B * P], endr[:, :], None, ALU.is_ge))
                V.scalar_tensor_tensor(out=R, in0=iota[:, 0:B * P], scalar=Xi[:, MAXK:MAXK + 1], in1=R,
                                       op0=ALU.is_ge, op1=ALU.subtract).then_inc(r_ready, 1)

            def col(ap, n, k):
                return ap.rearrange("p (b o) -> p b o", o=1).broadcast_to([P, n, k])

            def edges(i):
                t, r, F, K, GR, B = plan.groups[i]
                at, n0 = plan.at[i], plan.block0[i]
                bl = slice(n0, n0 + B)
                dve.wait_ge(sel_done, i + 1)
                sel = ps[:, 2 + i % 2, 0:B * (K + MW)].rearrange("p (b w) -> p b w", b=B)
                step(V.tensor_copy(meta[:, bl, :], sel[:, :, K:K + 3]))
                V.tensor_copy(sq[:, at:at + B, :], sel[:, :, K + 3:K + 7])
                V.tensor_scalar(rowq[:, bl], meta[:, bl, 2], -1.0, None, ALU.add).then_inc(chain, 1)
                ch.n += 1
                step(V.tensor_tensor(kq[:, bl], qpos[:, 0:B], meta[:, bl, 0], ALU.subtract))
                eqi = eq[:, i % 4, 0:B * K].rearrange("p (b k) -> p b k", b=B)
                pr = prod[:, 0:B * K].rearrange("p (b k) -> p b k", b=B)
                step(V.tensor_tensor(eqi, iota[:, 0:K].rearrange("p (o k) -> p o k", o=1).broadcast_to([P, B, K]),
                                     col(kq[:, bl], B, K), ALU.is_equal))
                step(V.tensor_tensor(pr, eqi, sel[:, :, 0:K], ALU.mult))
                step(V.tensor_reduce(jq[:, 0:B], pr, AX, ALU.add))
                V.tensor_scalar(idx[:, bl], jq[:, 0:B], -1.0, 0.0, ALU.add, ALU.max).then_inc(idx_ready, 1)
                V.tensor_tensor(OQ[:, at:at + B, :], iota[:, 0:P].rearrange("p (o k) -> p o k", o=1).broadcast_to([P, B, P]),
                                col(rowq[:, bl], B, P), ALU.is_equal)

            def scores(i):
                t, r, F, K, GR, B = plan.groups[i]
                at = plan.at[i]
                dve.wait_ge(gathered[i % 4], gat_need[i])
                ei = e[:, at:at + B, :]
                step(V.tensor_tensor(ei, sq[:, at:at + B, :], G[:, at:at + B, D:D + H], ALU.add))
                step(V.scalar_tensor_tensor(out=ei, in0=ei, scalar=ALPHA, in1=ei, op0=ALU.mult, op1=ALU.max))
                if i >= 1:
                    dve.wait_ge(rowe_done, i)
                for b in range(B):
                    last = V.tensor_tensor(E2[:, b * K * H:(b + 1) * K * H].rearrange("p (k h) -> p k h", h=H),
                                           eq[:, i % 4, b * K:(b + 1) * K].rearrange("p (k o) -> p k o", o=1).broadcast_to([P, K, H]),
                                           ei[:, b:b + 1, :].broadcast_to([P, K, H]), ALU.mult)
                last.then_inc(e2_ready, 1)

            def group_max(i):
                t, r, F, K, GR, B = plan.groups[i]
                dve.wait_ge(rowe_done, i + 1)
                step(V.tensor_scalar(valid[:, i % 8, 0:K], valid[:, i % 8, 0:K], -1.0, BIG, ALU.add, ALU.mult))
                step(V.tensor_tensor(em[:, 0:K, :], ps[:, 5, 0:K * H].rearrange("p (k h) -> p k h", h=H),
                                     col(valid[:, i % 8, 0:K], K, H), ALU.add))
                o = mv[:, r, :] if F > 1 else mrow[:, t % 2, :]
                last = V.tensor_reduce(o, em[:, 0:K, :].rearrange("p k h -> p h k"), AX, ALU.max)
                if F > 1:
                    step(last)
                    if r == F - 1:
                        last = V.tensor_reduce(mrow[:, t % 2, :], mv[:, 0:F, :].rearrange("p v h -> p h v"), AX, ALU.max)
                if r == F - 1:
                    last.then_inc(max_ready, 1)

            def less_max(t):
                dve.wait_ge(mback_done, t + 1)
                nblk = 0
                for v in range(plan.first[t], plan.last[t] + 1):
                    B, at = plan.groups[v][5], plan.at[v]
                    step(V.tensor_tensor(dq[:, at:at + B, :], e[:, at:at + B, :],
                                         ps[:, 4, nblk * H:(nblk + B) * H].rearrange("p (b h) -> p b h", h=H), ALU.subtract))
                    V.tensor_scalar(dq[:, at:at + B, :], dq[:, at:at + B, :], 0.0, None, ALU.min).then_inc(d_ready, 1)
                    nblk += B

            def weigh(t):
                for v in range(plan.first[t], plan.last[t] + 1):
                    B, at = plan.groups[v][5], plan.at[v]
                    dve.wait_ge(p_ready, v + 1)
                    for b in range(B):
                        g = G[:, at + b, 0:D].rearrange("p (h d) -> p h d", h=H)
                        last = V.tensor_tensor(g, g, col(G[:, at + b, D:D + H], H, HD), ALU.mult)
                    last.then_inc(g_ready, 1)

            def finish(t):
                dve.wait_ge(agg_done, t + 1)
                o = ps[:, 6 + t % 2, :]
                if t == 0:
                    dve.wait_ge(mean_ready, 1)
                step(V.tensor_tensor(rc2[:, :], rc[:, t, 0:1], rc[:, t, 1:2], ALU.add))
                step(V.tensor_scalar(none[:, t:t + 1], rc2[:, :], 0.0, None, ALU.is_equal))
                step(V.tensor_scalar(den[:, :], o[:, D:D + H], none[:, t:t + 1], None, ALU.add))
                step(V.reciprocal(rden[:, :], den[:, :]))
                V.tensor_tensor(hp[:, :].rearrange("p (h d) -> p h d", h=H), o[:, 0:D].rearrange("p (h d) -> p h d", h=H),
                                col(rden[:, :], H, HD), ALU.mult).then_inc(agg_used, 1)
                dve.wait_ge(agg_used, t + 1)
                step(V.scalar_tensor_tensor(out=hp[:, :], in0=mwh[:, :], scalar=none[:, t:t + 1], in1=hp[:, :],
                                            op0=ALU.mult, op1=ALU.add))
                V.tensor_scalar(mn[:, :], hp[:, :], 0.0, None, ALU.min).then_inc(elu_in, 1)
                dve.wait_ge(elu_out, t + 1)
                step(V.scalar_tensor_tensor(out=hp[:, :], in0=hp[:, :], scalar=0.0, in1=ex[:, :], op0=ALU.max, op1=ALU.add))
                step(V.scalar_tensor_tensor(out=xs[:, t, :], in0=hp[:, :], scalar=-1.0, in1=xs[:, t, :], op0=ALU.add, op1=ALU.add))
                step(V.bn_stats(stats[:, t, :], xs[:, t, :]))
                step(V.bn_aggr(agg[:, t, :], stats[:, t, :]))
                V.tensor_scalar(veps[:, t:t + 1], agg[:, t, 1:2], EPS, None, ALU.add).then_inc(var1_ready, 1)
                V.tensor_scalar(hn[:, t, :], xs[:, t, :], agg[:, t, 0:1], 0.0, ALU.subtract, ALU.max).then_inc(c1_ready, 1)

            for g in range(T // 4):
                dve.wait_ge(whx_ready, 4 * g + 4)
                V.tensor_copy(s_all[:, 4 * g:4 * g + 4, :], whx[:, g % 2, :, D + H:D + 2 * H]).then_inc(s_copied, 1)
            dve.wait_ge(s_copied, T // 4)
            for i in range(NV + 6):
                if i < NV:
                    extract(i)
                if 0 <= i - 3 < NV:
                    group_max(i - 3)
                if i < NV:
                    rows_of_edges(i)
                for t in plan.ended(i - 4):
                    less_max(t)
                if i < NV:
                    edges(i)
                for t in plan.ended(i - 4):
                    weigh(t)
                if 0 <= i - 2 < NV:
                    scores(i - 2)
                for t in plan.ended(i - 5):
                    finish(t)
            step(V.tensor_scalar(last_q[:, :], rowq[:, :], 0.0, None, ALU.is_ge))
            step(V.tensor_reduce(missed[:, 0:1], last_q[:, :], AX, ALU.add))
            step(V.tensor_reduce(missed[:, 1:2], rc[:, :, :].rearrange("p t c -> p (t c)"), AX, ALU.add))
            step(V.tensor_tensor(missed[:, 2:3], missed[:, 1:2], missed[:, 0:1], ALU.subtract))
            step(V.tensor_scalar(keep[:, :], kq[:, :], 0.0, None, ALU.is_gt))
            step(V.tensor_scalar(last_q[:, :], meta[:, :, 1], -1.0, None, ALU.add))
            step(V.tensor_tensor(last_q[:, :], last_q[:, :], kq[:, :], ALU.is_equal))

    def edge_max():
      with ExitStack() as ctx:
        def sbl(name, shape, dt=F32):
            return ctx.enter_context(nc.sbuf_tensor(name, shape, dt))

        def sem(name):
            return ctx.enter_context(nc.semaphore(name))
        NG = 8
        G1 = sbl("G1", [P, NG, P])
        dg = sbl("dg", [P, 3, P], BF16)
        ones = sbl("ones", [P, P], BF16)
        onesf = sbl("onesf", [P, P])
        Fl = sbl("Fl", [P, 3, P])
        S = sbl("S", [P, 3, P])
        Sb = sbl("Sb", [P, 3, P])
        OL = sbl("OL", [P, 3, P])
        pl = sbl("pl", [P, 2, P])
        found = [sem(f"g1_in{b}") for b in range(NG)]
        ones_ready, diag_ready, fps_done, fl_ready, tr_done = (sem("ones_ready"), sem("diag_ready"), sem("fps_done"),
                                                               sem("fl_ready"), sem("tr_done"))
        scan_done, back_done, sb_ready, ol_ready, pool_done, pool_used, out_ready, stored, miss_done, mchain = (
            sem("scan_done"), sem("back_done"), sem("sb_ready"), sem("ol_ready"), sem("pool_done"), sem("pool_used"),
            sem("out_ready"), sem("stored"), sem("miss_done"), sem("mchain"))
        block = ctx.enter_context(nc.Block("edges1"))
        LASTB = {plan.block0[i] + plan.groups[i][5] - 1: i for i in range(NV)}
        FIRSTB = {plan.block0[i]: i for i in range(NV)}

        @block.gpsimd
        def _(pool):
            for n in range(NB):
                if n >= NG:
                    pool.wait_ge(tr_done, n - NG + 1)
                pool.indirect_dma_start(G1[:, n % NG, :], None, h1_table,
                                        bass.IndirectOffsetOnAxis(ap=idx[:, n:n + 1], axis=0)).then_inc(found[n % NG], 16)

        @block.scalar
        def _(act):
            for n in range(NB + 3):
                if n < NB:
                    if n >= 3:
                        act.wait_ge(fps_done, n - 2)
                    nc.scalar.activation(dg[:, n % 3, :], identb[:, :], ACT.Copy, scale=keep[:, n:n + 1]).then_inc(diag_ready, 1)
                if 0 <= n - 1 < NB:
                    m = n - 1
                    act.wait_ge(fps_done, m + 1)
                    if m >= 3:
                        act.wait_ge(scan_done, m - 2)
                    nc.scalar.copy(Fl[:, m % 3, :], ps[:, 7 * (m % 2), 0:P]).then_inc(fl_ready, 1)
                if 0 <= n - 3 < NB:
                    m = n - 3
                    act.wait_ge(back_done, m + 1)
                    if m >= 3:
                        act.wait_ge(pool_done, m - 2)
                    nc.scalar.copy(Sb[:, m % 3, :], ps[:, 3 + m % 2, 0:P]).then_inc(sb_ready, 1)

        @block.tensor
        def _(pe):
            pe.wait_ge(ones_ready, 2)
            nc.tensor.matmul(ps[:, 6, 0:1], onesf[:, :], missed[:, 2:3], start=True, stop=True).then_inc(miss_done, 1)
            for n in range(NB + 4):
                if n < NB:
                    pe.wait_ge(diag_ready, n + 1)
                    if n >= 2:
                        pe.wait_ge(fl_ready, n - 1)
                    nc.tensor.matmul(ps[:, 7 * (n % 2), 0:P], ones[:, :], dg[:, n % 3, :], start=True, stop=True
                                     ).then_inc(fps_done, 1)
                if 0 <= n - 1 < NB:
                    m = n - 1
                    tile_in = m % NG
                    pe.wait_ge(found[tile_in], 16 * (m // NG + 1))
                    if m >= 2:
                        pe.wait_ge(scan_done, m - 1)
                    nc.tensor.transpose(ps[:, 1 + m % 2, 0:P], G1[:, m % NG, :], ident[:, :]).then_inc(tr_done, 1)
                if 0 <= n - 3 < NB:
                    m = n - 3
                    pe.wait_ge(scan_done, m + 1)
                    if m >= 2:
                        pe.wait_ge(sb_ready, m - 1)
                    nc.tensor.transpose(ps[:, 3 + m % 2, 0:P], S[:, m % 3, :], ident[:, :]).then_inc(back_done, 1)
                if 0 <= n - 4 < NB:
                    m = n - 4
                    i = max(v for v in range(NV) if plan.block0[v] <= m)
                    pe.wait_ge(sb_ready, m + 1)
                    pe.wait_ge(ol_ready, m + 1)
                    if m in FIRSTB and i >= 2:
                        pe.wait_ge(pool_used, i - 1)
                    nc.tensor.matmul(ps[:, 5 + i % 2, 0:P], OL[:, m % 3, :], Sb[:, m % 3, :],
                                     start=(m in FIRSTB), stop=(m in LASTB)).then_inc(pool_done, 1)

        @block.vector
        def _(dve):
            V = nc.vector
            ch = Chain(dve, mchain)
            V.memset(ones[:, :], 1.0).then_inc(ones_ready, 1)
            V.memset(onesf[:, :], 1.0).then_inc(ones_ready, 1)
            dve.wait_ge(miss_done, 1)
            ch.step(V.tensor_copy(missed[:, 3:4].bitcast(I32), ps[:, 6, 0:1]))
            for n in range(NB + 6):
                if n < NB:
                    dve.wait_ge(fl_ready, n + 1)
                    dve.wait_ge(tr_done, n + 1)
                    if n >= 3:
                        dve.wait_ge(back_done, n - 2)
                    if n:
                        dve.wait_ge(scan_done, n)
                    start = 0.0 if n in FIRSTB else S[:, (n - 1) % 3, P - 1:P]
                    V.tensor_tensor_scan(S[:, n % 3, :], Fl[:, n % 3, :], ps[:, 1 + n % 2, 0:P], start, ALU.mult, ALU.max
                                         ).then_inc(scan_done, 1)
                    if n >= 3:
                        dve.wait_ge(pool_done, n - 2)
                    V.tensor_scalar(OL[:, n % 3, :], iota[:, 0:P], rowq[:, n:n + 1], last_q[:, n:n + 1], ALU.is_equal, ALU.mult
                                    ).then_inc(ol_ready, 1)
                m = n - 5
                if m in LASTB:
                    i = LASTB[m]
                    t, r, F, K, GR, B = plan.groups[i]
                    dve.wait_ge(pool_done, m + 1)
                    o = ps[:, 5 + i % 2, 0:P]
                    if F > 1:
                        if r == 0:
                            last = V.tensor_copy(pl[:, 0, :], o)
                        else:
                            last = V.tensor_tensor(pl[:, 0, :], pl[:, 0, :], o, ALU.max)
                        last.then_inc(pool_used, 1)
                        dve.wait_ge(pool_used, i + 1)
                        if r == F - 1:
                            V.tensor_tensor(hn[:, t, :], pl[:, 0, :], xs[:, t, :], ALU.add).then_inc(out_ready, 1)
                    else:
                        V.tensor_tensor(hn[:, t, :], o, xs[:, t, :], ALU.add).then_inc(pool_used, 1)
                        dve.wait_ge(pool_used, i + 1)
                        V.tensor_copy(pl[0:1, 1, 0:1], xs[0:1, 0, 0:1]).then_inc(out_ready, 1)

        @block.sync
        def _(sp):
            for t in range(T):
                sp.wait_ge(pool_used, plan.last[t] + 1)
                sp.wait_ge(out_ready, t + 1)
                sp.dma_start(out_v[:, t, :], hn[:, t, :]).then_inc(stored, 16)
            sp.wait_ge(stored, 16 * T)

    edge_attention()
    edge_max()


def gnn_kernel(nc, x, adj, W, a, out):
    with ExitStack() as kept:
        missed = kept.enter_context(nc.sbuf_tensor("missed", [P, 4], F32))
        with ExitStack() as top:
            edge_path(nc, x, adj, W, a, out, top, missed)
        gap = nc.values_load(missed[0:1, 3:4].bitcast(I32), min_val=0, max_val=1 << 24)
        with nc.If(gap > 0):
            general_path(nc, x, adj, W, a, out)


_INS = ['x', 'adj', 'L0_gnn_W', 'L0_gnn_a']
_OUTS = [((4096, 128), 'float32')]


def kernel(**inputs):
    import numpy as _np
    import concourse.bacc as _bacc
    from concourse import mybir as _mybir
    from concourse.bass_utils import run_bass_kernel_spmd as _run

    nc = _bacc.Bacc("TRN2", target_bir_lowering=False, num_devices=1)
    arrays, args = {}, []
    for name in _INS:
        a = _np.ascontiguousarray(inputs[name])
        arrays[f"in_{name}_dram"] = a
        args.append(nc.dram_tensor(f"in_{name}_dram", a.shape, _mybir.dt.from_np(a.dtype), kind="ExternalInput").ap())
    for i, (shape, dtype) in enumerate(_OUTS):
        dt = _mybir.dt.from_np(_np.dtype(dtype))
        args.append(nc.dram_tensor(f"out_{i}_dram", shape, dt, kind="ExternalOutput").ap())
    gnn_kernel(nc, *args)
    r = _run(nc, [arrays], core_ids=[0])
    got = tuple(r.results[0][f"out_{i}_dram"] for i in range(len(_OUTS)))
    return got[0]
```

```python
from contextlib import ExitStack

import concourse.bass as bass
from concourse import mybir

F32 = mybir.dt.float32
I32 = mybir.dt.int32
I16 = mybir.dt.int16
BF16 = mybir.dt.bfloat16
F16 = mybir.dt.float16
ALU = mybir.AluOpType
ACT = mybir.ActivationFunctionType
AX = mybir.AxisListType.X
P = 128
ALPHA = 0.2
NEG_INF = -9000000000000000.0
EPS = 1e-05


class Chain:

    def __init__(self, eng, sem, base=0):
        self.eng, self.sem, self.base, self.n = eng, sem, base, 0

    def step(self, ins):
        self.n += 1
        ins.then_inc(self.sem, 1)
        self.eng.wait_ge(self.sem, self.base + self.n)


def general_path(nc, x, adj, W, a, out):
    N, D = x.shape
    H = a.shape[1]
    HD = a.shape[2] // 2
    T = N // P
    TG = 4
    NGRP = T // TG
    WX = D + 2 * H
    x_v = x.rearrange("(t p) d -> p t d", p=P)
    out_v = out.rearrange("(t p) d -> p t d", p=P)

    with ExitStack() as top:
        def sb(name, shape, dt=F32):
            return top.enter_context(nc.sbuf_tensor(name, shape, dt))

        ps = top.enter_context(nc.psum_tensor("ps", [P, 8, 512], F32))
        ident = sb("ident", [P, P])
        wx = sb("wx", [P, WX])
        abc = sb("abc", [P, 2 * D])
        wa = sb("wa", [P, H, 2, HD])
        wab = sb("wab", [P, H, P])
        xs = sb("xs", [P, T, D])
        hn = sb("hn", [P, T, D])
        hT = sb("hT", [P, N])
        whx = sb("whx", [P, T, WX])
        st = sb("st", [P, 4, T])
        tb = sb("tb", [P, H, N])
        adjt = sb("adjt", [P, N], I32)
        negm = sb("negm", [P, N])
        u = sb("u", [P, N])
        pT = sb("pT", [P, 2, 512])
        scur = sb("scur", [P, H])
        nmax = sb("nmax", [P, H])
        rsum = sb("rsum", [P, H])
        rinv = sb("rinv", [P, H])
        hp = sb("hp", [P, D])
        pooled = sb("pooled", [P, 8])

        def layernorm(tag, load_x):
            with ExitStack() as ctx:
                def sem(name):
                    return ctx.enter_context(nc.semaphore(f"{tag}_{name}"))
                x_in = sem("x_in"); w_in = sem("w_in"); chain = sem("chain"); id0 = sem("id0"); id1 = sem("id1")
                sq_done = sem("sq_done"); var_ready = sem("var_ready"); std_ready = sem("std_ready")
                centred = sem("centred"); h_ready = sem("h_ready")
                tr_done = sem("tr_done"); hT_ready = sem("hT_ready")
                wx_ready = sem("wx_ready"); mm_done = sem("mm_done"); whx_ready = sem("whx_ready")
                block = ctx.enter_context(nc.Block(tag))

                @block.sync
                def _(sp):
                    if load_x:
                        sp.dma_start(wx[:, 0:D], W).then_inc(w_in, 16)
                        sp.dma_start(abc[:, :], a.rearrange("o h k -> o (h k)").broadcast_to([P, 2 * D])).then_inc(w_in, 16)
                        sp.dma_start(xs[:, :, :], x_v).then_inc(x_in, 16)

                @block.gpsimd
                def _(pool):
                    if load_x:
                        nc.gpsimd.memset(ident[:, :], 0.0).then_inc(id0, 1)
                        pool.wait_ge(id0, 1)
                        nc.gpsimd.affine_select(out=ident[:, :], in_=ident[:, :], compare_op=ALU.not_equal, fill=1.0,
                                                base=0, pattern=[[-1, P]], channel_multiplier=1).then_inc(id1, 1)

                G = 8
                NC_ = T // G

                @block.vector
                def _(dve):
                    ch = Chain(dve, chain)
                    if load_x:
                        dve.wait_ge(w_in, 32)
                        for k in range(2):
                            ch.step(nc.vector.tensor_tensor(
                                wa[:, :, k, :], abc[:, :].rearrange("p (h s d) -> p h s d", h=H, s=2)[:, :, k, :],
                                wx[:, 0:D].rearrange("p (h d) -> p h d", h=H), ALU.mult))
                        nc.vector.tensor_reduce(wx[:, D:D + H], wa[:, :, 1, :], AX, ALU.add).then_inc(wx_ready, 1)
                        nc.vector.tensor_reduce(wx[:, D + H:D + 2 * H], wa[:, :, 0, :], AX, ALU.add).then_inc(wx_ready, 1)
                        dve.wait_ge(wx_ready, 2)
                        nc.vector.tensor_copy(wab[:, :, :], wx[:, D:D + H].rearrange("p (h o) -> p h o", o=1).broadcast_to([P, H, P])).then_inc(wx_ready, 1)
                        dve.wait_ge(x_in, 16)
                    for c in range(NC_):
                        g = slice(c * G, c * G + G)
                        ch.step(nc.vector.tensor_reduce(st[:, 0, g], xs[:, g, :], AX, ALU.add))
                        ch.step(nc.vector.tensor_scalar(st[:, 0, g], st[:, 0, g], 1.0 / D, None, ALU.mult))
                        nc.vector.tensor_tensor(hn[:, g, :], xs[:, g, :],
                                                st[:, 0, g].rearrange("p (t o) -> p t o", o=1).broadcast_to([P, G, D]),
                                                ALU.subtract).then_inc(centred, 1)
                        dve.wait_ge(sq_done, c + 1)
                        ch.step(nc.vector.tensor_reduce(st[:, 1, g], u[:, c * G * D:(c + 1) * G * D].rearrange("p (t d) -> p t d", d=D), AX, ALU.add))
                        nc.vector.tensor_scalar(st[:, 2, g], st[:, 1, g], 1.0 / D, EPS, ALU.mult, ALU.add).then_inc(var_ready, 1)
                        dve.wait_ge(std_ready, c + 1)
                        ch.step(nc.vector.reciprocal(st[:, 2, g], st[:, 3, g]))
                        nc.vector.scalar_tensor_tensor(
                            out=hn[:, g, :], in0=hn[:, g, :], scalar=0.0,
                            in1=st[:, 2, g].rearrange("p (t o) -> p t o", o=1).broadcast_to([P, G, D]),
                            op0=ALU.max, op1=ALU.mult).then_inc(h_ready, 1)

                @block.scalar
                def _(act):
                    for c in range(NC_):
                        g = slice(c * G, c * G + G)
                        act.wait_ge(centred, c + 1)
                        nc.scalar.activation(u[:, c * G * D:(c + 1) * G * D], hn[:, g, :].rearrange("p t d -> p (t d)"),
                                             ACT.Square).then_inc(sq_done, 1)
                        act.wait_ge(var_ready, c + 1)
                        nc.scalar.activation(st[:, 3, g], st[:, 2, g], ACT.Sqrt).then_inc(std_ready, 1)
                    for g in range(NGRP):
                        act.wait_ge(tr_done, g + 1)
                        nc.scalar.copy(hT[:, g * 512:(g + 1) * 512], ps[:, g % 2, :]).then_inc(hT_ready, 1)
                        if load_x:
                            act.wait_ge(mm_done, g + 1)
                            nc.scalar.copy(whx[:, g * TG:g * TG + TG, :].rearrange("p (b k) w -> p b (k w)", b=2),
                                           ps[:, 2 + 2 * (g % 2):4 + 2 * (g % 2), 0:2 * WX]).then_inc(whx_ready, 1)
                    if load_x:
                        for h in range(H):
                            for c in range(N // 512):
                                act.wait_ge(mm_done, NGRP + h * (N // 512) + c + 1)
                                nc.scalar.copy(tb[:, h, c * 512:(c + 1) * 512], ps[:, 6 + c % 2, :]).then_inc(whx_ready, 1)

                @block.tensor
                def _(pe):
                    if load_x:
                        pe.wait_ge(id1, 1)
                        pe.wait_ge(wx_ready, 3)
                    for g in range(NGRP):
                        pe.wait_ge(h_ready, g * TG // G + 1)
                        if g >= 2:
                            pe.wait_ge(hT_ready, g - 1)
                        for k in range(TG):
                            last = nc.tensor.transpose(ps[:, g % 2, k * P:(k + 1) * P], hn[:, g * TG + k, :], ident[:, :])
                        last.then_inc(tr_done, 1)
                        if load_x:
                            pe.wait_ge(hT_ready, g + 1)
                            if g >= 2:
                                pe.wait_ge(whx_ready, g - 1)
                            for k in range(TG):
                                last = nc.tensor.matmul(ps[:, 2 + 2 * (g % 2) + k // 2, (k % 2) * WX:(k % 2 + 1) * WX],
                                                        hT[:, (g * TG + k) * P:(g * TG + k + 1) * P], wx[:, :], start=True, stop=True)
                            last.then_inc(mm_done, 1)
                    if load_x:
                        for h in range(H):
                            for c in range(N // 512):
                                n = h * (N // 512) + c
                                if n >= 2:
                                    pe.wait_ge(whx_ready, NGRP + n - 1)
                                nc.tensor.matmul(ps[:, 6 + c % 2, :], wab[:, h, :], hT[:, c * 512:(c + 1) * 512],
                                                 start=True, stop=True).then_inc(mm_done, 1)

        def dense_attention():
            with ExitStack() as ctx:
                def sem(name):
                    return ctx.enter_context(nc.semaphore(f"g0_{name}"))
                adj_in = sem("adj_in"); x_in = sem("x_in"); chain = sem("chain"); e_ready = sem("e_ready"); p_ready = sem("p_ready")
                pT_done = sem("pT_done"); pT_ready = sem("pT_ready"); acc_done = sem("acc_done"); tile_done = sem("tile_done")
                elu_in = sem("elu_in"); elu_out = sem("elu_out")
                block = ctx.enter_context(nc.Block("g0"))
                C = T // 4
                STEPS = 2 + H * 6 + 4

                @block.sync
                def _(sp):
                    with sp.Fori(0, T) as t:
                        sp.wait_ge(tile_done, t + 1)
                        sp.dma_start(adjt[:, :], adj[bass.ds(t * P, P), :]).then_inc(adj_in, 16)

                @block.vector
                def _(dve):
                    nc.vector.memset(hp[:, :], 0.0).then_inc(tile_done, 1)
                    dve.wait_ge(tile_done, 1)
                    with dve.Fori(0, T) as t:
                        ch = Chain(dve, chain, t * STEPS)
                        ch.step(nc.vector.tensor_scalar(scur[:, :], whx[:, bass.ds(t, 1), D + H:D + 2 * H].rearrange("p o h -> p (o h)"), 1.0, None, ALU.mult))
                        dve.wait_ge(adj_in, t * 16 + 16)
                        ch.step(nc.vector.tensor_scalar(negm[:, :], adjt[:, :], -NEG_INF, NEG_INF, ALU.mult, ALU.add))
                        for h in range(H):
                            ch.step(nc.vector.tensor_scalar(u[:, :], tb[:, h, :], scur[:, h:h + 1], None, ALU.add))
                            ch.step(nc.vector.scalar_tensor_tensor(out=u[:, :], in0=u[:, :], scalar=ALPHA, in1=u[:, :],
                                                                   op0=ALU.mult, op1=ALU.max))
                            ch.step(nc.vector.tensor_tensor(u[:, :], u[:, :], adjt[:, :], ALU.mult))
                            ch.step(nc.vector.tensor_tensor(u[:, :], u[:, :], negm[:, :], ALU.add))
                            nc.vector.tensor_reduce(nmax[:, h:h + 1], u[:, :], AX, ALU.max, negate=True).then_inc(e_ready, 1)
                            dve.wait_ge(p_ready, t * H + h + 1)
                            ch.step(nc.vector.reciprocal(rinv[:, h:h + 1], rsum[:, h:h + 1]))
                            dve.wait_ge(acc_done, t * H + h + 1)
                            ch.step(nc.vector.tensor_scalar(hp[:, h * HD:(h + 1) * HD], ps[:, 4, 0:HD], rinv[:, h:h + 1], None, ALU.mult))
                        xt = xs[:, bass.ds(t, 1), :].rearrange("p o d -> p (o d)")
                        nc.vector.tensor_scalar(u[:, 0:D], hp[:, :], 0.0, None, ALU.min).then_inc(elu_in, 1)
                        dve.wait_ge(elu_out, t + 1)
                        ch.step(nc.vector.scalar_tensor_tensor(out=u[:, 0:D], in0=hp[:, :], scalar=0.0, in1=u[:, D:2 * D], op0=ALU.max, op1=ALU.add))
                        ch.step(nc.vector.tensor_scalar(u[:, 0:D], u[:, 0:D], -1.0, None, ALU.add))
                        ch.step(nc.vector.tensor_scalar(hp[:, :], xt, 1.0, None, ALU.mult))
                        ch.step(nc.vector.tensor_tensor(hp[:, :], hp[:, :], u[:, 0:D], ALU.add))
                        nc.vector.tensor_scalar(xt, hp[:, :], 1.0, None, ALU.mult).then_inc(tile_done, 1)
                        dve.wait_ge(tile_done, t + 2)

                @block.scalar
                def _(act):
                    with act.Fori(0, T) as t:
                        for h in range(H):
                            act.wait_ge(e_ready, t * H + h + 1)
                            nc.scalar.activation(u[:, :], u[:, :], ACT.Exp, bias=nmax[:, h:h + 1],
                                                 accum_out=rsum[:, h:h + 1]).then_inc(p_ready, 1)
                            for c in range(C):
                                n = h * C + c
                                act.wait_ge(pT_done, t * (H * C) + n + 1)
                                nc.scalar.copy(pT[:, n % 2, :], ps[:, n % 2, :]).then_inc(pT_ready, 1)
                        act.wait_ge(elu_in, t + 1)
                        nc.scalar.activation(u[:, D:2 * D], u[:, 0:D], ACT.Exp).then_inc(elu_out, 1)

                @block.tensor
                def _(pe):
                    with pe.Fori(0, T) as t:
                        for h in range(H):
                            pe.wait_ge(p_ready, t * H + h + 1)

                            def transposes(c):
                                n = h * C + c
                                for k in range(4):
                                    last = nc.tensor.transpose(ps[:, n % 2, k * P:(k + 1) * P],
                                                               u[:, (c * 4 + k) * P:(c * 4 + k + 1) * P], ident[:, :])
                                last.then_inc(pT_done, 1)

                            transposes(0)
                            for c in range(C):
                                n = h * C + c
                                if c + 1 < C:
                                    if n:
                                        pe.wait_ge(pT_ready, t * (H * C) + n)
                                    transposes(c + 1)
                                pe.wait_ge(pT_ready, t * (H * C) + n + 1)
                                for k in range(4):
                                    j = c * 4 + k
                                    last = nc.tensor.matmul(ps[:, 4, 0:HD], pT[:, n % 2, k * P:(k + 1) * P],
                                                            whx[:, j, h * HD:(h + 1) * HD], start=(j == 0), stop=(j == T - 1))
                            last.then_inc(acc_done, 1)

        def dense_max():
            with ExitStack() as ctx:
                def sem(name):
                    return ctx.enter_context(nc.semaphore(f"g1_{name}"))
                NB = 4
                mask_in = [sem(f"mask_in{b}") for b in range(NB)]
                row_done = sem("row_done"); copied = sem("copied"); tr_done = sem("tr_done"); summed = sem("summed"); out_done = sem("out_done")
                block = ctx.enter_context(nc.Block("g1"))
                outT = negm

                @block.sync
                def _(sp):
                    with sp.Fori(0, N // NB) as i:
                        for b in range(NB):
                            sp.wait_ge(copied, i * NB + NB)
                            sp.dma_start(tb[:, b, :].bitcast(I32), adj[bass.ds(i * NB + b, 1), :].broadcast_to([P, N])).then_inc(mask_in[b], 16)
                    sp.wait_ge(summed, T)
                    sp.dma_start(out_v, hn[:, :, :]).then_inc(out_done, 16)
                    sp.wait_ge(out_done, 16)

                @block.vector
                def _(dve):
                    nc.vector.memset(pooled[:, 0:NB], 0.0).then_inc(copied, NB)
                    dve.wait_ge(copied, NB)
                    with dve.Fori(0, N // NB) as i:
                        for b in range(NB):
                            dve.wait_ge(mask_in[b], i * 16 + 16)
                            nc.vector.memset(pooled[:, NB:NB + 1], 0.0)
                            nc.vector.tensor_tensor_reduce(out=u[:, :], in0=hT[:, :], in1=tb[:, b, :].bitcast(I32), scale=1.0, scalar=0.0,
                                                           op0=ALU.mult, op1=ALU.max, accum_out=pooled[:, b:b + 1]).then_inc(row_done, 1)
                            dve.wait_ge(row_done, i * NB + b + 1)
                        nc.vector.tensor_scalar(outT[:, bass.ds(i * NB, NB)], pooled[:, 0:NB], 1.0, None, ALU.mult).then_inc(copied, NB)
                        dve.wait_ge(copied, i * NB + 2 * NB)
                    for t in range(T):
                        dve.wait_ge(tr_done, t + 1)
                        nc.vector.tensor_tensor(hn[:, t, :], ps[:, t % 4, 0:D], xs[:, t, :], ALU.add).then_inc(summed, 1)

                @block.tensor
                def _(pe):
                    pe.wait_ge(copied, N + NB)
                    for t in range(T):
                        if t >= 4:
                            pe.wait_ge(summed, t - 3)
                        nc.tensor.transpose(ps[:, t % 4, 0:P], outT[:, t * P:(t + 1) * P], ident[:, :]).then_inc(tr_done, 1)

        layernorm("ln0", True)
        dense_attention()
        layernorm("ln1", False)
        dense_max()


def edge_batches(tiles):
    blocks = {1: 11, 2: 8, 3: 7, 4: 6, 5: 6}

    def unit(t):
        b = blocks.get(t, 5 if t < 10 else 4 if t < 18 else 3)
        return (t, 0, 1, 24 if t < 4 else 16, 8 if t < 4 else 4, b)

    hubs = [(0, r, 8, 32, 4, 3) for r in range(8)]
    cuts = [1, 2, 4, 7, 11, 16, 22, 28, tiles]
    return [hubs[0:4], hubs[4:8]] + [[unit(t) for t in range(a, b)] for a, b in zip(cuts, cuts[1:])]


BITS = 8
BIG = 1e30


class Plan:

    def __init__(self, tiles):
        self.batches = edge_batches(tiles)
        self.units = [u for b in self.batches for u in b]
        self.n, self.nb = len(self.units), len(self.batches)
        self.unit0, self.size, self.at, self.block0, self.free_after = [], [], [], [], []
        self.off = []
        self.unit_block0 = []
        n = un = 0
        for k, batch in enumerate(self.batches):
            size = sum(u[5] for u in batch)
            self.unit0.append(un)
            un += len(batch)
            self.size.append(size)
            self.block0.append(n)
            offs = [sum(u[5] for u in batch[:j]) for j in range(len(batch))]
            self.off.append(offs)
            self.unit_block0 += [n + o for o in offs]
            n += size
        users = [[0, 1]] + [[k] for k in range(2, self.nb)]
        room = [max(sum(self.size[k] for k in u) for u in users[s::3]) for s in range(3)]
        for i, user in enumerate(users):
            at = sum(room[:i % 3])
            for k in user:
                self.at.append(at)
                at += self.size[k]
                self.free_after.append(users[i - 3][-1] if i >= 3 else -1)
        self.ring = sum(room)
        self.word_at, self.word_room = [], 0
        for k, batch in enumerate(self.batches):
            at = 0 if k == self.nb - 1 else self.word_room
            for u in batch:
                self.word_at.append(at)
                at += 8 * u[4]
            self.word_room = max(self.word_room, at)
        self.blocks = n
        self.last = [max(i for i in range(self.n) if self.units[i][0] == t) for t in range(tiles)]
        self.batch_of_unit = [k for k, b in enumerate(self.batches) for _ in b]

    def whole(self, k):
        return [] if k == 0 or not 0 <= k < self.nb else [0, 1] if k == 1 else [k]

    def tiles(self, k):
        return sorted({u[0] for j in self.whole(k) for u in self.batches[j]})


def edge_path(nc, x, adj, W, a, out, top, missed):
    N, D = x.shape
    H = a.shape[1]
    HD = a.shape[2] // 2
    T = N // P
    WX = D + 2 * H
    C = N // BITS
    plan = Plan(T)
    RING = plan.ring
    NV, NB, NBT = plan.n, plan.blocks, plan.nb
    MAXB = max(g[5] for g in plan.units)
    MW = 7
    NA = 4
    wh_table = nc.dram_tensor("wh_table", [N, WX], F32).ap()
    h1_table = nc.dram_tensor("h1_table", [N, D], F32).ap()
    x_v = x.rearrange("(t p) d -> p t d", p=P)
    wh_v = wh_table.rearrange("(t p) d -> p t d", p=P)
    h1_v = h1_table.rearrange("(t p) d -> p t d", p=P)
    out_v = out.rearrange("(t p) d -> p t d", p=P)

    def sb(name, shape, dt=F32):
        return top.enter_context(nc.sbuf_tensor(name, shape, dt))

    ps = top.enter_context(nc.psum_tensor("psf", [P, 8, 512], F32))
    ident = sb("identf", [P, P])
    identb = sb("identb", [P, P], BF16)
    iota = sb("iota", [P, MAXB * P], I16)
    xs = sb("xsf", [P, T, D])
    idx = sb("idx", [P, NB], I32)
    meta = sb("meta", [P, NB, 3])
    kq = sb("kq", [P, NB])
    last_q = sb("last_q", [P, NB])
    keep = sb("keep", [P, NB])

    def edge_attention():
      with ExitStack() as ctx:
        def sbl(name, shape, dt=F32):
            return ctx.enter_context(nc.sbuf_tensor(name, shape, dt))

        def sem(name):
            return ctx.enter_context(nc.semaphore(name))
        U = max(len(b) for b in plan.batches)
        XW = max(len(b) * (b[0][3] + MW) for b in plan.batches)
        SK = max(sum(u[5] for u in b) * b[0][3] for b in plan.batches)
        UK = max(len(b) * b[0][3] for b in plan.batches)
        SIZE = max(plan.size)
        adjt = sbl("adjf", [P, NA, N // 2], I32)
        adjb = sbl("adjb", [P, 2, N], BF16)
        Rm = sbl("Rm", [P, RING, P], BF16)
        OQ = sbl("OQ", [P, RING, P])
        G = sbl("G", [P, RING, WX])
        near = sbl("near", [P, 2, MAXB * P], I16)
        slots = sbl("slots", [P, 32], I16)
        hn = G[:, 0:T, 0:D]
        whsum = G[:, 40:44, 0:D]
        hTb = OQ[:, 0:8, :]
        whx = OQ[:, 24:24 + -(-T * WX // P), :].rearrange("p a b -> p (a b)")[:, 0:T * WX].rearrange("p (t w) -> p t w", w=WX)
        tri = sbl("tri", [P, P])
        packw = sbl("packw", [P, BITS, P], BF16)
        ones_b = sbl("ones_b", [1, P], BF16)
        cnum = sbl("cnum", [1, C], F16)
        avg = sbl("avg", [P, P])
        maskk = sbl("maskk", [P, BITS], I32)
        qpos = sbl("qpos", [P, MAXB])
        rown = sbl("rown", [P, 1])
        X = sbl("X", [P, 2, XW])
        Xr = sbl("Xr", [P, XW])
        Xb = sbl("Xb", [P, 3, XW], BF16)
        s_all = sbl("s_all", [P, T, H])
        wd = sbl("wd", [P, plan.word_room])
        wi = sbl("wi", [P, UK], I32)
        cand = sbl("cand", [P, UK * BITS], I32)
        valid = sbl("valid", [P, 3, UK])
        some = sbl("some", [P, U])
        ends = sbl("ends", [P, 2, U])
        eq = sbl("eq", [P, 2, SK], BF16)
        sq = sbl("sq", [P, RING, H])
        jq = sbl("jq", [P, 5, SIZE])
        e = sbl("e", [P, RING, H])
        dq = sbl("dq", [P, RING, H])
        E2 = sbl("E2", [P, SK * H])
        em = sbl("em", [P, UK, H])
        prod = E2[:, 0:SK]
        wsel = em[:, :, :].rearrange("p k h -> p (k h)")
        mv = sbl("mv", [P, 8, H])
        mrow = sbl("mrow", [P, U, H])
        mrem = sbl("mrem", [P, U, H])
        m3 = sbl("m3", [P, 2, U, 3, H], BF16)
        rc = sbl("rc", [P, T, 2])
        none = sbl("none", [P, T])
        ag = sbl("ag", [P, U, D + H])
        den = sbl("den", [P, U, H])
        hp = sbl("hp_f", [P, U, D])
        mn = sbl("mn", [P, U, D])
        ex = mn
        h1b = sbl("h1b", [P, 2, U, D])
        mwh = sbl("mwh", [P, D])
        stats = sbl("stats", [P, T, 6])
        agg = sbl("agg", [P, T, 2])
        veps = sbl("veps", [P, T])
        rstd = sbl("rstd", [P, T])
        half = sbl("half", [P, T])
        bias = sbl("bias", [P, T])
        wx = OQ[:, 60:62, :].rearrange("p a b -> p (a b)")[:, 0:WX]
        abc = OQ[:, 8:10, :].rearrange("p a b -> p (a b)")
        wa = OQ[:, 10:12, :].rearrange("p a b -> p (a b)").rearrange("p (h s d) -> p h s d", h=H, s=2)

        w_in, x_in = sem("w_in"), [sem(f"x_in{c}") for c in range(4)]
        adj_in = [sem(f"adj_in{b}") for b in range(NA)]
        adj_bf, packed, words_used = sem("adj_bf"), sem("packed"), sem("words_used")
        consts, pchain, chain = sem("consts"), sem("pchain"), sem("chain")
        packw_ready, wx_ready = sem("packw_ready"), sem("wx_ready")
        var0_ready, rstd0_ready, c0_ready = sem("var0_ready"), sem("rstd0_ready"), sem("c0_ready")
        tr0_done, hT_ready, mm0_done, whx_ready = sem("tr0_done"), sem("hT_ready"), sem("mm0_done"), sem("whx_ready")
        wh_stored, ident_ready, summed, c0_pool = sem("wh_stored"), sem("ident_ready"), sem("summed"), sem("c0_pool")
        mean_done, mean_ready, s_copied = sem("mean_done"), sem("mean_ready"), sem("s_copied")
        x_ready, off_done, r_ready, xb_ready = sem("x_ready"), sem("off_done"), sem("r_ready"), sem("xb_ready")
        sel_done, oqt_done, oq_ready, idx_ready = sem("sel_done"), sem("oqt_done"), sem("oq_ready"), sem("idx_ready")
        gathered = [sem(f"gathered{b}") for b in range(2)]
        e2_ready, rowe_done, max_ready, mback_done = sem("e2_ready"), sem("rowe_done"), sem("max_ready"), sem("mback_done")
        d_ready, p_ready, g_ready, agg_done = sem("d_ready"), sem("p_ready"), sem("g_ready"), sem("agg_done")
        ag_ready, ag_used, g_pool = sem("ag_ready"), sem("ag_used"), sem("g_pool")
        elu_in, elu_out, var1_ready, rstd1_ready = sem("elu_in"), sem("elu_out"), sem("var1_ready"), sem("rstd1_ready")
        h1_ready, h1_stored = sem("h1_ready"), [sem(f"h1_stored{b}") for b in range(2)]
        block = ctx.enter_context(nc.Block("edges0"))

        oq_n = [0]
        for k in range(NBT):
            oq_n.append(oq_n[-1] + -(-plan.size[k] // 8))
        gat_need, tot = [], [0, 0]
        for k in range(NBT):
            tot[k % 2] += 16 * plan.size[k]
            gat_need.append(tot[k % 2])
        POINTS = 4
        POOL_LN = T // 8 - 1
        NCONST = 1 + BITS + 7 + 1

        def pool_tiles(k):
            tl = plan.tiles(k)
            return tl[:len(tl) // 2] if len(tl) > 2 else []

        weighed_at, weighed_by = {}, [0, 0]
        for k in range(NBT):
            for t in plan.tiles(k):
                by = int(t in pool_tiles(k))
                weighed_by[by] += 1
                weighed_at[t] = ([g_ready, g_pool][by], weighed_by[by])

        TAKE = [2, 2, 3, 3, 3, 4, 5, 5]
        TAKE += [T - 1 - sum(TAKE)]

        def taken(k, j):
            if k < 0:
                return plan.last[0] + 1
            tiles = sum(TAKE[:k]) + (TAKE[k] * (j + 1) // POINTS if k < len(TAKE) else 0)
            return plan.last[min(tiles, T - 1)] + 1

        def words_free(k, j):
            n = taken(k, j)
            return min(max([t for t in range(T) if plan.last[t] < n], default=-1) + 2, T - 1)

        assert all(taken(k, POINTS - 1) >= plan.unit0[k + 1] + len(plan.batches[k + 1]) for k in range(NBT - 1))

        @block.sync
        def _(sp):
            sp.dma_start(wx[:, 0:D], W).then_inc(w_in, 16)
            sp.dma_start(abc[:, :], a.rearrange("o h k -> o (h k)").broadcast_to([P, 2 * D])).then_inc(w_in, 16)

            def load_adj(m):
                if m >= NA:
                    sp.wait_ge(adj_bf, m - NA + 1)
                t, c = m // 2, (m % 2) * (N // 2)
                sp.dma_start(adjt[:, m % NA, :], adj[t * P:(t + 1) * P, c:c + N // 2]).then_inc(adj_in[m % NA], 16)

            for c in range(4):
                g = slice(c * T // 4, (c + 1) * T // 4)
                sp.dma_start(xs[:, g, :], x_v[:, g, :]).then_inc(x_in[c], 16)
                if c in (1, 2):
                    load_adj(c - 1)
            for m in range(2, 2 * T):
                load_adj(m)

        @block.gpsimd
        def _(pool):
            ch = Chain(pool, pchain)
            ch.step(nc.gpsimd.memset(ident[:, :], 0.0))
            nc.gpsimd.affine_select(out=ident[:, :], in_=ident[:, :], compare_op=ALU.not_equal, fill=1.0,
                                    base=0, pattern=[[-1, P]], channel_multiplier=1).then_inc(ident_ready, 1)
            nc.gpsimd.memset(half[:, :], -0.5).then_inc(consts, 1)
            for k in range(BITS):
                nc.gpsimd.memset(maskk[:, k:k + 1], (1 << (9 + k)) + C - 1).then_inc(consts, 1)
            nc.gpsimd.iota(cnum[:, :], pattern=[[1, C]], base=0, channel_multiplier=0,
                           allow_small_or_imprecise_dtypes=True).then_inc(consts, 1)
            nc.gpsimd.memset(ones_b[:, :], 1.0).then_inc(consts, 1)
            nc.gpsimd.iota(qpos[:, :], pattern=[[P, MAXB]], base=0, channel_multiplier=1,
                           allow_small_or_imprecise_dtypes=True).then_inc(consts, 1)
            nc.gpsimd.iota(iota[:, :], pattern=[[1, MAXB * P]], base=1, channel_multiplier=0,
                           allow_small_or_imprecise_dtypes=True).then_inc(consts, 1)
            nc.gpsimd.iota(slots[:, :], pattern=[[1, 32]], base=0, channel_multiplier=0,
                           allow_small_or_imprecise_dtypes=True).then_inc(consts, 1)
            nc.gpsimd.iota(rown[:, :], pattern=[[0, 1]], base=1, channel_multiplier=1,
                           allow_small_or_imprecise_dtypes=True).then_inc(consts, 1)
            nc.gpsimd.memset(avg[:, :], 1.0 / N).then_inc(consts, 1)
            ch.step(nc.gpsimd.memset(tri[:, :], 1.0))
            nc.gpsimd.affine_select(out=tri[:, :], in_=tri[:, :], compare_op=ALU.is_gt, fill=0.0,
                                    base=0, pattern=[[1, P]], channel_multiplier=-1).then_inc(consts, 1)
            pool.wait_ge(consts, NCONST)
            for c in range(4):
                g = slice(c * T // 4, (c + 1) * T // 4)
                pool.wait_ge(var0_ready, c + 1)
                for t in range(c * T // 4, c * T // 4 + POOL_LN):
                    last = nc.gpsimd.tensor_scalar(hn[:, t, :], xs[:, t, :], agg[:, t, 0:1], 0.0, ALU.subtract, ALU.max)
                last.then_inc(c0_pool, 1)
                nc.gpsimd.tensor_tensor(rstd[:, g], veps[:, g], half[:, g], ALU.pow).then_inc(rstd0_ready, 1)
            for g in range(1, T // 4):
                pool.wait_ge(whx_ready, 4 * g + 4)
                nc.gpsimd.tensor_tensor(whsum, whx[:, 0:4, 0:D] if g == 1 else whsum, whx[:, 4 * g:4 * g + 4, 0:D], ALU.add
                                        ).then_inc(summed, 1)
                pool.wait_ge(summed, g)
            pool.wait_ge(wh_stored, 16 * (T // 4))
            for k in range(NBT + 4):
                for u, t in enumerate(pool_tiles(k - 2)):
                    pool.wait_ge(p_ready, k - 1)
                    at = plan.at[k - 2] + plan.off[k - 2][u]
                    n = plan.batches[k - 2][u][5]
                    g = G[:, at:at + n, 0:D].rearrange("p b (h d) -> p b h d", h=H)
                    nc.gpsimd.tensor_tensor(g, g, G[:, at:at + n, D:D + H].rearrange("p b (h o) -> p b h o", o=1).broadcast_to(
                        [P, n, H, HD]), ALU.mult).then_inc(g_pool, 1)
                if k < NBT:
                    pool.wait_ge(idx_ready, k + 1)
                    if plan.free_after[k] >= 0:
                        pool.wait_ge(agg_done, plan.tiles(plan.free_after[k])[-1] + 1)
                    for b in range(plan.size[k]):
                        n = plan.block0[k] + b
                        pool.indirect_dma_start(G[:, plan.at[k] + b, :], None, wh_table,
                                                bass.IndirectOffsetOnAxis(ap=idx[:, n:n + 1], axis=0)
                                                ).then_inc(gathered[k % 2], 16)
                tl = plan.tiles(k - 3)
                if tl:
                    pool.wait_ge(var1_ready, 2 * (k - 3))
                    g = slice(tl[0], tl[-1] + 1)
                    ch.step(nc.gpsimd.tensor_tensor(rstd[:, g], veps[:, g], half[:, g], ALU.pow))
                    nc.gpsimd.tensor_tensor(bias[:, g], bias[:, g], rstd[:, g], ALU.mult).then_inc(rstd1_ready, 1)

        @block.scalar
        def _(act):
            def convert(t):
                for m in (2 * t, 2 * t + 1):
                    act.wait_ge(adj_in[m % NA], 16 * (m // NA + 1))
                    if m % 2 == 0 and t >= 2:
                        act.wait_ge(packed, t - 1)
                    c = (m % 2) * (N // 2)
                    nc.scalar.activation(adjb[:, t % 2, c:c + N // 2], adjt[:, m % NA, :], ACT.Copy,
                                         accum_out=rc[:, t, m % 2:m % 2 + 1]).then_inc(adj_bf, 1)

            def wh_out(g):
                act.wait_ge(mm0_done, g + 1)
                if g % 2 == 0:
                    act.wait_ge(rstd0_ready, g // 2 + 1)
                for k in range(4):
                    t = 4 * g + k
                    w = ps[:, 2 + 2 * (g % 2) + k // 2, (k % 2) * WX:(k % 2 + 1) * WX]
                    nc.scalar.activation(whx[:, t, :], w, ACT.Copy, scale=rstd[:, t:t + 1]).then_inc(whx_ready, 1)

            def store_wh(g):
                act.wait_ge(whx_ready, 4 * g + 4)
                act.dma_start(wh_v[:, 4 * g:4 * g + 4, :], whx[:, 4 * g:4 * g + 4, :]).then_inc(wh_stored, 16)

            for g in range(T // 4 + 1):
                if g < T // 4:
                    act.wait_ge(tr0_done, g + 1)
                    if g >= 2:
                        act.wait_ge(mm0_done, g - 1)
                    nc.scalar.copy(hTb[:, 4 * (g % 2):4 * (g % 2) + 4, :], ps[:, 6 + g % 2, :].rearrange("p (k q) -> p k q", k=4)
                                   ).then_inc(hT_ready, 1)
                if g == 1:
                    convert(0)
                if g >= 1:
                    wh_out(g - 1)
                if g >= 2:
                    store_wh(g - 2)
            store_wh(T // 4 - 1)
            nc.scalar.copy(s_all[:, :, :], whx[:, :, D + H:D + 2 * H]).then_inc(s_copied, 1)
            converted = 0

            def convert_to(last):
                nonlocal converted
                while converted < min(last, T - 1):
                    converted += 1
                    convert(converted)

            convert_to(words_free(-1, POINTS - 1) + 2)
            for k in range(NBT + 4):
                convert_to(words_free(k, 0) + 2)
                f = k - 4
                tl = plan.tiles(f)
                if tl:
                    act.wait_ge(rstd1_ready, f)
                    if f >= 3:
                        act.wait_ge(h1_stored[f % 2], 16 * ((f - 1) // 2))
                    for j, t in enumerate(tl):
                        nc.scalar.activation(h1b[:, f % 2, j, :], xs[:, t, :], ACT.Relu, bias=bias[:, t:t + 1],
                                             scale=rstd[:, t:t + 1]).then_inc(h1_ready, 1)
                    act.wait_ge(h1_ready, tl[-1] + 1)
                    act.dma_start(h1_v[:, tl[0]:tl[-1] + 1, :], h1b[:, f % 2, 0:len(tl), :]).then_inc(h1_stored[f % 2], 16)
                if k < NBT:
                    for j in range(0, plan.size[k], 8):
                        nb = min(8, plan.size[k] - j)
                        act.wait_ge(oqt_done, oq_n[k] + j // 8 + 1)
                        nc.scalar.copy(OQ[:, plan.at[k] + j:plan.at[k] + j + nb, :],
                                       ps[:, 5 - 2 * ((oq_n[k] + j // 8) % 2), :].bitcast(BF16)[:, 0:nb * P].rearrange("p (b q) -> p b q", q=P)
                                       ).then_inc(oq_ready, 1)
                for j in plan.whole(k - 2):
                    act.wait_ge(d_ready, j + 1)
                    bl = slice(plan.at[j], plan.at[j] + plan.size[j])
                    nc.scalar.activation(G[:, bl, D:D + H], dq[:, bl, :], ACT.Exp).then_inc(p_ready, 1)
                convert_to(words_free(k, 1) + 2)
                f = k - 3
                tl = plan.tiles(f)
                if tl:
                    act.wait_ge(elu_in, f)
                    nc.scalar.activation(ex[:, 0:len(tl), :], mn[:, 0:len(tl), :], ACT.Exp).then_inc(elu_out, 1)
                convert_to(words_free(k, 2) + 2)
                if k == 1:
                    act.wait_ge(wh_stored, 16 * (T // 4))
                    act.wait_ge(mean_done, 1)
                    nc.scalar.copy(mwh[:, :], ps[:, 7, 0:D]).then_inc(mean_ready, 1)
                for j, t in enumerate(plan.tiles(k - 2)):
                    act.wait_ge(agg_done, t + 1)
                    if k - 3 >= 1:
                        act.wait_ge(ag_used, k - 3)
                    nc.scalar.copy(ag[:, j, :], ps[:, 6 + t % 2, 0:D + H]).then_inc(ag_ready, 1)
                convert_to(words_free(k, 3) + 2)
            for b in range(2):
                act.wait_ge(h1_stored[b], 16 * len(range(2 - b, NBT, 2)))

        @block.tensor
        def _(pe):
            def pack(t):
                pe.wait_ge(adj_bf, 2 * t + 2)
                if t >= 2:
                    pe.wait_ge(words_used, plan.last[t - 2] + 1)
                o = ps[:, t % 2, :]
                for k in range(BITS):
                    nc.tensor.matmul(o, packw[:, k, :], adjb[:, t % 2, k * C:(k + 1) * C], start=(k == 0), stop=False)
                nc.tensor.matmul(o, ones_b[:, :], cnum[:, :], start=False, stop=True).then_inc(packed, 1)

            def means():
                pe.wait_ge(summed, T // 4 - 1)
                for k in range(4):
                    last = nc.tensor.matmul(ps[:, 7, 0:D], avg[:, :], whsum[:, k, :], start=(k == 0), stop=(k == 3))
                last.then_inc(mean_done, 1)

            pe.wait_ge(ident_ready, 1)
            pe.wait_ge(wx_ready, 2)
            for g in range(T // 4 + 1):
                if g < T // 4:
                    if g % 2 == 0:
                        pe.wait_ge(c0_ready, g // 2 + 1)
                        pe.wait_ge(c0_pool, g // 2 + 1)
                    if g >= 2:
                        pe.wait_ge(hT_ready, g - 1)
                    for k in range(4):
                        last = nc.tensor.transpose(ps[:, 6 + g % 2, k * P:(k + 1) * P], hn[:, 4 * g + k, :], ident[:, :])
                    last.then_inc(tr0_done, 1)
                if g >= 1:
                    m = g - 1
                    pe.wait_ge(hT_ready, m + 1)
                    if m >= 2:
                        pe.wait_ge(whx_ready, 4 * (m - 1))
                    for k in range(4):
                        last = nc.tensor.matmul(ps[:, 2 + 2 * (m % 2) + k // 2, (k % 2) * WX:(k % 2 + 1) * WX],
                                                hTb[:, 4 * (m % 2) + k, :], wx[:, :], start=True, stop=True)
                    last.then_inc(mm0_done, 1)
                if g == 2:
                    pe.wait_ge(consts, NCONST)
                    pe.wait_ge(packw_ready, BITS + 1)
                    pack(0)
            pe.wait_ge(hT_ready, T // 4)
            pe.wait_ge(whx_ready, T)
            packs = 0

            def pack_to(last):
                nonlocal packs
                while packs < last:
                    packs += 1
                    pack(packs)

            for k in range(NBT + 2):
                K = plan.batches[min(k, NBT - 1)][0][3]
                if k < NBT:
                    pe.wait_ge(x_ready, k + 1)
                    nu = len(plan.batches[k])
                    Xk = X[:, k % 2, 0:nu * (K + MW)].rearrange("p (u w) -> p u w", u=nu)
                    nc.tensor.matmul(ps[:, 2, 512 - nu:512], tri[:, :], Xk[:, :, K + 1], start=True, stop=True).then_inc(off_done, 1)
                pack_to(words_free(k, 0))
                if plan.whole(k - 2):
                    pe.wait_ge(max_ready, k - 2)
                    nblk = 0
                    for j in plan.whole(k - 2):
                        for u, unit in enumerate(plan.batches[j]):
                            for b in range(unit[5]):
                                last = nc.tensor.matmul(ps[:, 4, nblk * 12:nblk * 12 + 12], Rm[:, plan.at[j] + plan.off[j][u] + b, :],
                                                        m3[:, (k + 1) % 2, u if k > 3 else 0, :, :].rearrange("p a h -> p (a h)"),
                                                        start=True, stop=True)
                                nblk += 1
                    last.then_inc(mback_done, 1)
                if k < NBT:
                    pe.wait_ge(r_ready, k + 1)
                    pe.wait_ge(xb_ready, k + 1)
                    for u, unit in enumerate(plan.batches[k]):
                        for b in range(unit[5]):
                            o = plan.off[k][u] + b
                            for part in range(3):
                                last = nc.tensor.matmul(ps[:, 2, o * (K + MW):(o + 1) * (K + MW)], Rm[:, plan.at[k] + o, :],
                                                        Xb[:, part, u * (K + MW):(u + 1) * (K + MW)],
                                                        start=(part == 0), stop=(part == 2))
                    last.then_inc(sel_done, 1)
                    for j in range(0, plan.size[k], 8):
                        n = oq_n[k] + j // 8
                        if n >= 2:
                            pe.wait_ge(oq_ready, n - 1)
                        for b in range(j, min(j + 8, plan.size[k])):
                            last = nc.tensor.transpose(ps[:, 5 - 2 * (n % 2), :].bitcast(BF16)[:, (b - j) * P:(b - j + 1) * P],
                                                       Rm[:, plan.at[k] + b, :], identb[:, :])
                        last.then_inc(oqt_done, 1)
                if k == 0:
                    means()
                pack_to(words_free(k, 1))
                pack_to(words_free(k, 2))
                if 0 <= k - 1 < NBT:
                    j = k - 1
                    Kj = plan.batches[j][0][3]
                    pe.wait_ge(e2_ready, j + 1)
                    pe.wait_ge(oq_ready, oq_n[j + 1])
                    for u, unit in enumerate(plan.batches[j]):
                        for b in range(unit[5]):
                            o = plan.off[j][u] + b
                            last = nc.tensor.matmul(ps[:, 4, u * Kj * H:(u + 1) * Kj * H], OQ[:, plan.at[j] + o, :],
                                                    E2[:, o * Kj * H:(o + 1) * Kj * H], start=(b == 0), stop=(b == unit[5] - 1))
                    last.then_inc(rowe_done, 1)
                for t in plan.tiles(k - 2):
                    pe.wait_ge(*weighed_at[t])
                    if t >= 2:
                        pe.wait_ge(ag_ready, t - 1)
                    blocks = [plan.at[j] + plan.off[j][u] + b for j in plan.whole(k - 2)
                              for u, unit in enumerate(plan.batches[j]) if unit[0] == t for b in range(unit[5])]
                    for n, b in enumerate(blocks):
                        last = nc.tensor.matmul(ps[:, 6 + t % 2, 0:D + H], OQ[:, b, :], G[:, b, 0:D + H],
                                                start=(n == 0), stop=(n == len(blocks) - 1))
                    last.then_inc(agg_done, 1)
                pack_to(words_free(k, 3))

        @block.vector
        def _(dve):
            ch = Chain(dve, chain)
            step = ch.step
            V = nc.vector

            def mark(ins):
                ch.n += 1
                ins.then_inc(chain, 1)
                return ch.n

            def need(n):
                dve.wait_ge(chain, n)

            def apart(ins):
                n = mark(ins)
                yield
                need(n)

            def together(*stages):
                stages = list(stages)
                while stages:
                    stages = [st for st in stages if next(st, True) is None]

            def spread(ap, n, k):
                return ap.rearrange("p (b o) -> p b o", o=1).broadcast_to([P, n, k])

            dve.wait_ge(ident_ready, 1)
            for k in range(BITS):
                V.tensor_scalar(packw[:, k, :], ident[:, :], float(1 << (9 + k)), None, ALU.mult).then_inc(packw_ready, 1)
            V.tensor_copy(identb[:, :], ident[:, :]).then_inc(packw_ready, 1)
            dve.wait_ge(w_in, 32)
            ab = abc[:, :].rearrange("p (h s d) -> p h s d", h=H, s=2)
            for k in range(2):
                n = mark(V.tensor_tensor(wa[:, :, k, :], ab[:, :, k, :], wx[:, 0:D].rearrange("p (h d) -> p h d", h=H), ALU.mult))
            need(n)
            V.tensor_reduce(wx[:, D:D + H], wa[:, :, 1, :], AX, ALU.add).then_inc(wx_ready, 1)
            V.tensor_reduce(wx[:, D + H:D + 2 * H], wa[:, :, 0, :], AX, ALU.add).then_inc(wx_ready, 1)
            for c in range(4):
                dve.wait_ge(x_in[c], 16)
                ts = range(c * T // 4, (c + 1) * T // 4)
                for t in ts:
                    n = mark(V.bn_stats(stats[:, t, :], xs[:, t, :]))
                need(n)
                for t in ts:
                    n = mark(V.bn_aggr(agg[:, t, :], stats[:, t, :]))
                need(n)
                g = slice(ts[0], ts[-1] + 1)
                V.tensor_scalar(veps[:, g], agg[:, g, 1], EPS, None, ALU.add).then_inc(var0_ready, 1)
                for t in ts[POOL_LN:]:
                    last = V.tensor_scalar(hn[:, t, :], xs[:, t, :], agg[:, t, 0:1], 0.0, ALU.subtract, ALU.max)
                last.then_inc(c0_ready, 1)
            dve.wait_ge(consts, NCONST)

            words_at = {}

            def take_words(k, j):
                for v in range(0 if k < 0 else taken(k, j - 1), taken(k, j)):
                    t, r, F, _, GR, _ = plan.units[v]
                    b = plan.batch_of_unit[v]
                    at = plan.word_at[v]
                    dve.wait_ge(packed, t + 1)
                    words = ps[:, t % 2, :].rearrange("p (m g f) -> p f g m", g=GR, f=F)
                    for g in range(GR):
                        last = V.max(wd[:, at + g * 8:at + g * 8 + 8], words[:, r, g, :])
                        if g < GR - 1:
                            words_at[b] = mark(last)
                    last.then_inc(words_used, 1)

            def extract(k):
                batch = plan.batches[k]
                nu, K, GR = len(batch), batch[0][3], batch[0][4]
                wdk = wd[:, plan.word_at[plan.unit0[k]]:][:, 0:nu * 8 * GR].rearrange("p (u w) -> p u w", u=nu)
                dve.wait_ge(words_used, plan.unit0[k] + nu)
                yield
                need(words_at[k])
                if 8 * GR > K:
                    for q in range(K // 8):
                        for u in range(nu):
                            n = mark(V.max(wsel[:, u * K + 8 * q:u * K + 8 * q + 8], wdk[:, u, :]))
                        if q < K // 8 - 1:
                            for u in range(nu):
                                yield
                                need(n - nu + 1 + u)
                                m = mark(V.match_replace(wdk[:, u, :], wsel[:, u * K + 8 * q:u * K + 8 * q + 8],
                                                         wdk[:, u, :], 0.0))
                            yield
                            need(m)
                    yield
                    need(n)
                    src = wsel[:, 0:nu * K].rearrange("p (u k) -> p u k", u=nu)
                else:
                    src = wdk[:, :, 0:K]
                yield from apart(V.tensor_copy(wi[:, 0:nu * K].rearrange("p (u k) -> p u k", u=nu), src))
                cnd = cand[:, 0:nu * K * BITS]
                yield from apart(V.tensor_tensor(cnd.rearrange("p (k b) -> p k b", b=BITS), spread(wi[:, 0:nu * K], nu * K, BITS),
                                     maskk[:, :].rearrange("p (o k) -> p o k", o=1).broadcast_to([P, nu * K, BITS]), ALU.bitwise_and))
                if k >= 2:
                    dve.wait_ge(off_done, k - 1)
                Xk = X[:, k % 2, 0:nu * (K + MW)].rearrange("p (u w) -> p u w", u=nu)
                for q in range(K // 8):
                    for u in range(nu):
                        n = mark(V.max(Xk[:, u, 8 * q:8 * q + 8], cnd[:, u * K * BITS:(u + 1) * K * BITS]))
                    if q < K // 8 - 1:
                        for u in range(nu):
                            yield
                            need(n - nu + 1 + u)
                            m = mark(V.match_replace(cnd[:, u * K * BITS:(u + 1) * K * BITS], Xk[:, u, 8 * q:8 * q + 8],
                                                     cnd[:, u * K * BITS:(u + 1) * K * BITS], 0.0))
                        yield
                        need(m)
                yield
                need(n)
                vk = valid[:, k % 3, 0:nu * K].rearrange("p (u k) -> p u k", u=nu)
                yield from apart(V.tensor_scalar(vk, Xk[:, :, 0:K], float(C), None, ALU.is_ge))
                mark(V.tensor_copy(Xk[:, :, K + 2], rown[:, :].broadcast_to([P, nu])))
                V.tensor_reduce(Xk[:, :, K + 1], vk, AX, ALU.add).then_inc(x_ready, 1)

            def rows_of_edges(k):
                batch = plan.batches[k]
                nu, K = len(batch), batch[0][3]
                W_ = nu * (K + MW)
                Xk = X[:, k % 2, 0:W_].rearrange("p (u w) -> p u w", u=nu)
                t0 = batch[0][0]
                s_k = s_all[:, t0:t0 + 1, :].broadcast_to([P, nu, H]) if batch[0][2] > 1 else s_all[:, t0:t0 + nu, :]
                if k == 0:
                    dve.wait_ge(s_copied, 1)
                mark(V.tensor_copy(Xk[:, :, K + 3:K + 7], s_k))
                dve.wait_ge(off_done, k + 1)
                mark(V.tensor_copy(Xk[:, :, K], ps[:, 2, 512 - nu:512]))
                n = mark(V.tensor_scalar(some[:, 0:nu], Xk[:, :, K + 1], 1.0, None, ALU.min))
                mark(V.tensor_tensor(ends[:, 1, 0:nu], ps[:, 2, 512 - nu:512], Xk[:, :, K + 1], ALU.add))
                yield
                need(n)
                mark(V.scalar_tensor_tensor(out=ends[:, 0, 0:nu], in0=ps[:, 2, 512 - nu:512], scalar=1.0, in1=some[:, 0:nu],
                                            op0=ALU.add, op1=ALU.mult))
                yield
                need(n + 1)
                yield from apart(V.tensor_tensor(ends[:, 1, 0:nu], ends[:, 1, 0:nu], some[:, 0:nu], ALU.mult))
                if plan.free_after[k] >= 0:
                    dve.wait_ge(agg_done, plan.tiles(plan.free_after[k])[-1] + 1)
                if k:
                    dve.wait_ge(sel_done, k)
                Xf = X[:, k % 2, 0:W_]
                yield from apart(V.tensor_copy(Xb[:, 0, 0:W_], Xf))
                yield from apart(V.tensor_tensor(Xr[:, 0:W_], Xf, Xb[:, 0, 0:W_], ALU.subtract))
                yield from apart(V.tensor_copy(Xb[:, 1, 0:W_], Xr[:, 0:W_]))
                V.tensor_tensor(Xb[:, 2, 0:W_], Xr[:, 0:W_], Xb[:, 1, 0:W_], ALU.subtract).then_inc(xb_ready, 1)
                made, used = {}, {}
                for p0 in range(0, nu, 2):
                    pair = range(p0, min(p0 + 2, nu))
                    for u in pair:
                        B = batch[u][5]
                        if p0:
                            yield
                            need(used[u - 2])
                        made[u] = mark(V.tensor_scalar(near[:, u % 2, 0:B * P], iota[:, 0:B * P], ends[:, 0, u:u + 1], ends[:, 1, u:u + 1],
                                                        ALU.max, ALU.min))
                    for u in pair:
                        B = batch[u][5]
                        at = plan.at[k] + plan.off[k][u]
                        yield
                        need(made[u])
                        ins = V.tensor_tensor(Rm[:, at:at + B, :].rearrange("p b q -> p (b q)"), near[:, u % 2, 0:B * P],
                                              iota[:, 0:B * P], ALU.is_equal)
                        if u < nu - 1:
                            used[u] = mark(ins)
                ins.then_inc(r_ready, 1)

            def edges(k):
                batch = plan.batches[k]
                nu, K, S = len(batch), batch[0][3], plan.size[k]
                bl = slice(plan.block0[k], plan.block0[k] + S)
                at = slice(plan.at[k], plan.at[k] + S)
                dve.wait_ge(sel_done, k + 1)
                sel = ps[:, 2, 0:S * (K + MW)].rearrange("p (b w) -> p b w", b=S)
                n = mark(V.tensor_copy(meta[:, bl, :], sel[:, :, K:K + 3]))
                mark(V.tensor_copy(sq[:, at, :], sel[:, :, K + 3:K + 7]))
                yield
                need(n)
                for u, unit in enumerate(batch):
                    ub = slice(plan.block0[k] + plan.off[k][u], plan.block0[k] + plan.off[k][u] + unit[5])
                    n = mark(V.tensor_tensor(kq[:, ub], qpos[:, 0:unit[5]], meta[:, ub, 0], ALU.subtract))
                yield
                need(n)
                eqk = eq[:, k % 2, 0:S * K].rearrange("p (b k) -> p b k", b=S)
                pr = prod[:, 0:S * K].rearrange("p (b k) -> p b k", b=S)
                yield from apart(V.tensor_tensor(eqk, slots[:, 0:K].rearrange("p (o k) -> p o k", o=1).broadcast_to([P, S, K]),
                                     spread(kq[:, bl], S, K), ALU.is_equal))
                yield from apart(V.tensor_tensor(pr, eqk, sel[:, :, 0:K], ALU.mult))
                yield from apart(V.tensor_reduce(jq[:, 0, 0:S], pr, AX, ALU.add))
                n = mark(V.tensor_copy(jq[:, 1, 0:S].bitcast(I32), jq[:, 0, 0:S]))
                m = mark(V.tensor_scalar(jq[:, 2, 0:S].bitcast(I32), jq[:, 0, 0:S].bitcast(I32), 23, None, ALU.logical_shift_right))
                yield
                need(n)
                yield from apart(V.tensor_scalar(jq[:, 3, 0:S].bitcast(I32), jq[:, 1, 0:S].bitcast(I32), C - 1, None, ALU.bitwise_and))
                yield from apart(V.scalar_tensor_tensor(out=jq[:, 4, 0:S], in0=jq[:, 2, 0:S].bitcast(I32), scalar=float(C),
                                            in1=jq[:, 3, 0:S].bitcast(I32), op0=ALU.mult, op1=ALU.add))
                V.tensor_scalar(idx[:, bl], jq[:, 4, 0:S], -float((127 + 9) * C), 0.0, ALU.add, ALU.max).then_inc(idx_ready, 1)

            def scores(k):
                K, S = plan.batches[k][0][3], plan.size[k]
                at = slice(plan.at[k], plan.at[k] + S)
                dve.wait_ge(gathered[k % 2], gat_need[k])
                yield from apart(V.tensor_tensor(e[:, at, :], sq[:, at, :], G[:, at, D:D + H], ALU.add))
                yield from apart(V.scalar_tensor_tensor(out=e[:, at, :], in0=e[:, at, :], scalar=ALPHA, in1=e[:, at, :], op0=ALU.mult, op1=ALU.max))
                eqk = eq[:, k % 2, 0:S * K].rearrange("p (b k o) -> p b k o", b=S, o=1).broadcast_to([P, S, K, H])
                ek = e[:, at, :].rearrange("p b (o h) -> p b o h", o=1).broadcast_to([P, S, K, H])
                V.tensor_tensor(E2[:, 0:S * K * H].rearrange("p (b k h) -> p b k h", b=S, k=K), eqk, ek, ALU.mult
                                ).then_inc(e2_ready, 1)

            def maxima(k):
                batch = plan.batches[k]
                nu, K = len(batch), batch[0][3]
                vk = valid[:, k % 3, 0:nu * K]
                yield from apart(V.tensor_scalar(vk, vk, -1.0, BIG, ALU.add, ALU.mult))
                dve.wait_ge(rowe_done, k + 1)
                emk = em[:, 0:nu * K, :]
                yield from apart(V.tensor_tensor(emk, ps[:, 4, 0:nu * K * H].rearrange("p (k h) -> p k h", h=H), spread(vk, nu * K, H), ALU.add))
                o = mv[:, 4 * k:4 * k + nu, :] if k < 2 else mrow[:, 0:nu, :]
                yield from apart(V.tensor_reduce(o, emk.rearrange("p (u k) h -> p u h k", u=nu), AX, ALU.max))
                if k == 0:
                    return
                if k == 1:
                    nu = 1
                    yield from apart(V.tensor_reduce(mrow[:, 0, :], mv[:, :, :].rearrange("p v h -> p h v"), AX, ALU.max))
                mr, mm, m_ = mrow[:, 0:nu, :], mrem[:, 0:nu, :], m3[:, (k + 1) % 2, 0:nu, :, :]
                yield from apart(V.tensor_copy(m_[:, :, 0, :], mr))
                yield from apart(V.tensor_tensor(mm, mr, m_[:, :, 0, :], ALU.subtract))
                yield from apart(V.tensor_copy(m_[:, :, 1, :], mm))
                V.tensor_tensor(m_[:, :, 2, :], mm, m_[:, :, 1, :], ALU.subtract).then_inc(max_ready, 1)

            def less_max(k):
                dve.wait_ge(mback_done, k)
                n0 = 0
                for j in plan.whole(k):
                    S = plan.size[j]
                    at = slice(plan.at[j], plan.at[j] + S)
                    mb_ = ps[:, 4, n0 * 12:(n0 + S) * 12].rearrange("p (b a h) -> p b h a", b=S, a=3)
                    yield from apart(V.tensor_reduce(dq[:, at, :], mb_, AX, ALU.add))
                    yield from apart(V.tensor_tensor(dq[:, at, :], e[:, at, :], dq[:, at, :], ALU.subtract))
                    V.tensor_scalar(dq[:, at, :], dq[:, at, :], 0.0, None, ALU.min).then_inc(d_ready, 1)
                    n0 += S

            def weigh(k):
                for j in plan.whole(k):
                    dve.wait_ge(p_ready, j + 1)
                    for u, unit in enumerate(plan.batches[j]):
                        if unit[0] in pool_tiles(j):
                            continue
                        at = plan.at[j] + plan.off[j][u]
                        bl = slice(at, at + unit[5])
                        g = G[:, bl, 0:D].rearrange("p b (h d) -> p b h d", h=H)
                        last = V.tensor_tensor(g, g, G[:, bl, D:D + H].rearrange("p b (h o) -> p b h o", o=1).broadcast_to(
                            [P, unit[5], H, HD]), ALU.mult)
                        if k > 1 or (j == 1 and u == len(plan.batches[1]) - 1):
                            last.then_inc(g_ready, 1)
                        yield

            def finish(k):
                tl = plan.tiles(k)
                nt = len(tl)
                g = slice(tl[0], tl[-1] + 1)
                if k == 1:
                    dve.wait_ge(mean_ready, 1)
                yield from apart(V.tensor_reduce(none[:, g], rc[:, g, :], AX, ALU.add))
                yield from apart(V.tensor_scalar(none[:, g], none[:, g], 0.0, None, ALU.is_equal))
                dve.wait_ge(ag_ready, tl[-1] + 1)
                yield from apart(V.tensor_scalar(den[:, 0:nt, :], ag[:, 0:nt, D:D + H], 0.5, None, ALU.max))
                yield from apart(V.reciprocal(den[:, 0:nt, :], den[:, 0:nt, :]))
                V.tensor_tensor(hp[:, 0:nt, :].rearrange("p t (h d) -> p t h d", h=H),
                                ag[:, 0:nt, 0:D].rearrange("p t (h d) -> p t h d", h=H),
                                den[:, 0:nt, :].rearrange("p t (h o) -> p t h o", o=1).broadcast_to([P, nt, H, HD]),
                                ALU.mult).then_inc(ag_used, 1)
                dve.wait_ge(ag_used, k)
                for j, t in enumerate(tl):
                    n = mark(V.scalar_tensor_tensor(out=hp[:, j, :], in0=mwh[:, :], scalar=none[:, t:t + 1], in1=hp[:, j, :],
                                                    op0=ALU.mult, op1=ALU.add))
                yield
                need(n)
                V.tensor_scalar(mn[:, 0:nt, :], hp[:, 0:nt, :], 0.0, None, ALU.min).then_inc(elu_in, 1)

            def finish_rest(k):
                tl = plan.tiles(k)
                nt = len(tl)
                g = slice(tl[0], tl[-1] + 1)
                dve.wait_ge(elu_out, k)
                flat = lambda ap: ap.rearrange("p t d -> p (t d)")
                yield from apart(V.scalar_tensor_tensor(out=flat(hp[:, 0:nt, :]), in0=flat(hp[:, 0:nt, :]), scalar=0.0, in1=flat(ex[:, 0:nt, :]),
                                            op0=ALU.max, op1=ALU.add))
                yield from apart(V.scalar_tensor_tensor(out=flat(xs[:, g, :]), in0=flat(hp[:, 0:nt, :]), scalar=-1.0, in1=flat(xs[:, g, :]),
                                            op0=ALU.add, op1=ALU.add))
                for t in tl:
                    n = mark(V.bn_stats(stats[:, t, :], xs[:, t, :]))
                yield
                need(n)
                for t in tl:
                    n = mark(V.bn_aggr(agg[:, t, :], stats[:, t, :]))
                yield
                need(n)
                V.tensor_scalar(veps[:, g], agg[:, g, 1], EPS, None, ALU.add).then_inc(var1_ready, 1)
                V.tensor_scalar(bias[:, g], agg[:, g, 0], -1.0, None, ALU.mult).then_inc(var1_ready, 1)

            def when(there, stage, k):
                return [stage(k)] if there else []

            take_words(-1, POINTS - 1)

            for k in range(NBT + 4):
                new = k < NBT
                together(*when(new, extract, k), *when(plan.tiles(k - 4), finish_rest, k - 4))
                take_words(k, 0)
                together(*when(0 <= k - 2 < NBT, maxima, k - 2), *when(new, rows_of_edges, k))
                take_words(k, 1)
                together(*when(plan.whole(k - 2), less_max, k - 2), *when(new, edges, k), *when(plan.tiles(k - 3), finish, k - 3))
                take_words(k, 2)
                together(*when(0 <= k - 1 < NBT, scores, k - 1), *when(plan.whole(k - 2), weigh, k - 2))
                take_words(k, 3)
            step(V.tensor_scalar(last_q[:, :], meta[:, :, 2], 0.0, None, ALU.is_gt))
            step(V.tensor_reduce(missed[:, 0:1], last_q[:, :], AX, ALU.add))
            step(V.tensor_reduce(missed[:, 1:2], rc[:, :, :].rearrange("p t c -> p (t c)"), AX, ALU.add))
            step(V.tensor_tensor(missed[:, 2:3], missed[:, 1:2], missed[:, 0:1], ALU.subtract))
            step(V.tensor_scalar(keep[:, :], kq[:, :], 0.0, None, ALU.is_gt))
            step(V.tensor_scalar(last_q[:, :], meta[:, :, 1], -1.0, None, ALU.add))
            step(V.tensor_tensor(last_q[:, :], last_q[:, :], kq[:, :], ALU.is_equal))

    def edge_max():
      with ExitStack() as ctx:
        def sbl(name, shape, dt=F32):
            return ctx.enter_context(nc.sbuf_tensor(name, shape, dt))

        def sem(name):
            return ctx.enter_context(nc.semaphore(name))
        NG = 12
        rows_out = sbl("rows_out", [P, T, D])
        G1 = sbl("G1", [P, NG, P])
        dg = sbl("dg", [P, 3, P], BF16)
        ones = sbl("ones", [P, P], BF16)
        onesf = sbl("onesf", [P, P])
        Fl = sbl("Fl", [P, 3, P])
        S = sbl("S", [P, 5, P])
        Sb = sbl("Sb", [P, 4, P])
        OL = sbl("OL", [P, 6, P])
        pl = sbl("pl", [P, 1, P])
        found = [sem(f"g1_in{b}") for b in range(NG)]
        ones_ready, diag_ready, fps_done, fl_ready, tr_done = (sem("ones_ready"), sem("diag_ready"), sem("fps_done"),
                                                               sem("fl_ready"), sem("tr_done"))
        scan_done, back_done, sb_ready, ol_ready, pool_done, pool_used, out_ready, stored, miss_done, mchain = (
            sem("scan_done"), sem("back_done"), sem("sb_ready"), sem("ol_ready"), sem("pool_done"), sem("pool_used"),
            sem("out_ready"), sem("stored"), sem("miss_done"), sem("mchain"))
        block = ctx.enter_context(nc.Block("edges1"))
        LASTB = {plan.unit_block0[i] + plan.units[i][5] - 1: i for i in range(NV)}
        FIRSTB = {plan.unit_block0[i]: i for i in range(NV)}

        @block.gpsimd
        def _(pool):
            for n in range(NB):
                if n >= NG:
                    pool.wait_ge(tr_done, n - NG + 1)
                pool.indirect_dma_start(G1[:, n % NG, :], None, h1_table,
                                        bass.IndirectOffsetOnAxis(ap=idx[:, n:n + 1], axis=0)).then_inc(found[n % NG], 16)

        @block.scalar
        def _(act):
            for n in range(NB + 4):
                if n < NB:
                    if n >= 3:
                        act.wait_ge(fps_done, n - 2)
                    nc.scalar.activation(dg[:, n % 3, :], identb[:, :], ACT.Copy, scale=keep[:, n:n + 1]).then_inc(diag_ready, 1)
                if 0 <= n - 1 < NB:
                    m = n - 1
                    act.wait_ge(fps_done, m + 1)
                    if m >= 3:
                        act.wait_ge(scan_done, m - 2)
                    nc.scalar.copy(Fl[:, m % 3, :], ps[:, 7 * (m % 2), 0:P]).then_inc(fl_ready, 1)
                if 0 <= n - 4 < NB:
                    m = n - 4
                    act.wait_ge(back_done, m + 1)
                    if m >= 4:
                        act.wait_ge(pool_done, m - 3)
                    nc.scalar.copy(Sb[:, m % 4, :], ps[:, 3 + m % 2, 0:P]).then_inc(sb_ready, 1)

        @block.tensor
        def _(pe):
            pe.wait_ge(ones_ready, 2)
            nc.tensor.matmul(ps[:, 6, 0:1], onesf[:, :], missed[:, 2:3], start=True, stop=True).then_inc(miss_done, 1)
            for n in range(NB + 5):
                if n < NB:
                    pe.wait_ge(diag_ready, n + 1)
                    if n >= 2:
                        pe.wait_ge(fl_ready, n - 1)
                    nc.tensor.matmul(ps[:, 7 * (n % 2), 0:P], ones[:, :], dg[:, n % 3, :], start=True, stop=True
                                     ).then_inc(fps_done, 1)
                if 0 <= n - 1 < NB:
                    m = n - 1
                    pe.wait_ge(found[m % NG], 16 * (m // NG + 1))
                    if m >= 2:
                        pe.wait_ge(scan_done, m - 1)
                    nc.tensor.transpose(ps[:, 1 + m % 2, 0:P], G1[:, m % NG, :], ident[:, :]).then_inc(tr_done, 1)
                if 0 <= n - 3 < NB:
                    m = n - 3
                    pe.wait_ge(scan_done, m + 1)
                    if m >= 2:
                        pe.wait_ge(sb_ready, m - 1)
                    nc.tensor.transpose(ps[:, 3 + m % 2, 0:P], S[:, m % 5, :], ident[:, :]).then_inc(back_done, 1)
                if 0 <= n - 5 < NB:
                    m = n - 5
                    i = max(v for v in range(NV) if plan.unit_block0[v] <= m)
                    pe.wait_ge(sb_ready, m + 1)
                    pe.wait_ge(ol_ready, m + 1)
                    if m in FIRSTB and i >= 2:
                        pe.wait_ge(pool_used, i - 1)
                    nc.tensor.matmul(ps[:, 5 + i % 2, 0:P], OL[:, m % 6, :], Sb[:, m % 4, :],
                                     start=(m in FIRSTB), stop=(m in LASTB)).then_inc(pool_done, 1)

        @block.vector
        def _(dve):
            V = nc.vector
            ch = Chain(dve, mchain)
            V.memset(ones[:, :], 1.0).then_inc(ones_ready, 1)
            V.memset(onesf[:, :], 1.0).then_inc(ones_ready, 1)
            dve.wait_ge(miss_done, 1)
            ch.step(V.tensor_copy(missed[:, 3:4].bitcast(I32), ps[:, 6, 0:1]))
            for n in range(NB + 7):
                if n < NB:
                    dve.wait_ge(fl_ready, n + 1)
                    dve.wait_ge(tr_done, n + 1)
                    if n >= 5:
                        dve.wait_ge(back_done, n - 4)
                    if n:
                        dve.wait_ge(scan_done, n)
                    start = 0.0 if n in FIRSTB else S[:, (n - 1) % 5, P - 1:P]
                    V.tensor_tensor_scan(S[:, n % 5, :], Fl[:, n % 3, :], ps[:, 1 + n % 2, 0:P], start, ALU.mult, ALU.max
                                         ).then_inc(scan_done, 1)
                    if n >= 6:
                        dve.wait_ge(pool_done, n - 5)
                    V.tensor_scalar(OL[:, n % 6, :], iota[:, 0:P], meta[:, n, 2:3], last_q[:, n:n + 1], ALU.is_equal, ALU.mult
                                    ).then_inc(ol_ready, 1)
                m = n - 6
                if m in LASTB:
                    i = LASTB[m]
                    t, r, F, K, GR, B = plan.units[i]
                    dve.wait_ge(pool_done, m + 1)
                    o = ps[:, 5 + i % 2, 0:P]
                    if F > 1:
                        if r == 0:
                            last = V.tensor_copy(pl[:, 0, :], o)
                        else:
                            last = V.tensor_tensor(pl[:, 0, :], pl[:, 0, :], o, ALU.max)
                        last.then_inc(pool_used, 1)
                        dve.wait_ge(pool_used, i + 1)
                        if r == F - 1:
                            V.tensor_tensor(rows_out[:, t, :], pl[:, 0, :], xs[:, t, :], ALU.add).then_inc(out_ready, 1)
                    else:
                        V.tensor_tensor(rows_out[:, t, :], o, xs[:, t, :], ALU.add).then_inc(pool_used, 1)

        @block.sync
        def _(sp):
            for t in range(T):
                sp.wait_ge(pool_used, plan.last[t] + 1)
                if t == 0:
                    sp.wait_ge(out_ready, 1)
                sp.dma_start(out_v[:, t, :], rows_out[:, t, :]).then_inc(stored, 16)
            sp.wait_ge(stored, 16 * T)

    edge_attention()
    edge_max()


def gnn_kernel(nc, x, adj, W, a, out):
    with ExitStack() as kept:
        missed = kept.enter_context(nc.sbuf_tensor("missed", [P, 4], F32))
        with ExitStack() as top:
            edge_path(nc, x, adj, W, a, out, top, missed)
        gap = nc.values_load(missed[0:1, 3:4].bitcast(I32), min_val=0, max_val=1 << 24)
        with nc.If(gap > 0):
            general_path(nc, x, adj, W, a, out)


_INS = ['x', 'adj', 'L0_gnn_W', 'L0_gnn_a']
_OUTS = [((4096, 128), 'float32')]


def kernel(**inputs):
    import numpy as _np
    import concourse.bacc as _bacc
    from concourse import mybir as _mybir
    from concourse.bass_utils import run_bass_kernel_spmd as _run

    nc = _bacc.Bacc("TRN2", target_bir_lowering=False, num_devices=1)
    arrays, args = {}, []
    for name in _INS:
        a = _np.ascontiguousarray(inputs[name])
        arrays[f"in_{name}_dram"] = a
        args.append(nc.dram_tensor(f"in_{name}_dram", a.shape, _mybir.dt.from_np(a.dtype), kind="ExternalInput").ap())
    for i, (shape, dtype) in enumerate(_OUTS):
        dt = _mybir.dt.from_np(_np.dtype(dtype))
        args.append(nc.dram_tensor(f"out_{i}_dram", shape, dt, kind="ExternalOutput").ap())
    gnn_kernel(nc, *args)
    r = _run(nc, [arrays], core_ids=[0])
    got = tuple(r.results[0][f"out_{i}_dram"] for i in range(len(_OUTS)))
    return got[0]
```
